# Optimizing a Trainium2 kernel written in Bass

```python
import numpy as np
import jax
import jax.numpy as jnp

def _softmax(x, axis=-1):
    return jax.nn.softmax(x, axis=axis)

def _gelu(x):
    return jax.nn.gelu(x, approximate=True)

def _silu(x):
    return jax.nn.silu(x)

def _sigmoid(x):
    return jax.nn.sigmoid(x)

def _layernorm(x, axis=-1, eps=1e-05):
    m = jnp.mean(x, axis=axis, keepdims=True)
    v = jnp.var(x, axis=axis, keepdims=True)
    return (x - m) / jnp.sqrt(v + eps)

def _scatter_add(tgt, idx, src, axis=0):
    return tgt.at[idx].add(src)

def _segment_sum(src, seg, n):
    return jax.ops.segment_sum(src, seg, n)
kernel_name = 'mk_seq_preln_d2_jaxref_r8_88d67a'

def setup_inputs(seed: int=0):
    np.random.seed(seed)
    _w = jnp.asarray

    def _L0_attn_setup():
        import jax, jax.numpy as jnp
        import numpy as np
        H = 8
        D = 64
        E = 128

        def sinusoidal_pe(T, d, dtype=jnp.float32):
            pos = jnp.arange(T, dtype=jnp.float32)[:, None]
            div = jnp.exp(jnp.arange(0, d, 2, dtype=jnp.float32) * (-np.log(10000.0) / d))
            ang = pos * div
            pe = jnp.stack([jnp.sin(ang), jnp.cos(ang)], axis=-1).reshape(T, d)
            return pe.astype(dtype)
        key = jax.random.key(seed)
        k1, k2, k3 = jax.random.split(key, 3)
        B, T = (2, 256)
        x = jax.random.normal(k1, (B, T, E), dtype=jnp.float32)
        Wqkv = jax.random.normal(k2, (3 * H * D, E), dtype=jnp.float32) * (1.0 / np.sqrt(E))
        Wo = jax.random.normal(k3, (E, H * D), dtype=jnp.float32) * (1.0 / np.sqrt(H * D))
        return {'x': x, 'Wqkv': Wqkv, 'Wo': Wo}
    _L0_attn_in = _L0_attn_setup()

    def _L0_ffn_setup():
        import jax, jax.numpy as jnp
        import numpy as np
        B, S, D, F, E = (4, 256, 128, 512, 8)
        key = jax.random.key(seed)
        ks = jax.random.split(key, 7)
        s1 = 1.0 / np.sqrt(D)
        s2 = 1.0 / np.sqrt(F)
        x = jax.random.normal(ks[0], (B, S, D), dtype=jnp.float32)
        W1 = jax.random.uniform(ks[1], (E, D, F), jnp.float32, -s1, s1)
        b1 = jax.random.uniform(ks[2], (E, F), jnp.float32, -s1, s1)
        W2 = jax.random.uniform(ks[3], (E, F, D), jnp.float32, -s2, s2)
        b2 = jax.random.uniform(ks[4], (E, D), jnp.float32, -s2, s2)
        Wr = jax.random.uniform(ks[5], (D, E), jnp.float32, -s1, s1)
        br = jax.random.uniform(ks[6], (E,), jnp.float32, -s1, s1)
        return {'x': x, 'W1': W1, 'b1': b1, 'W2': W2, 'b2': b2, 'Wr': Wr, 'br': br}
    _L0_ffn_in = _L0_ffn_setup()

    def _L1_attn_setup():
        import jax, jax.numpy as jnp
        import numpy as np
        N_HEAD = 16
        EPS = 1e-06

        def _linear_attention(q, k, v):
            B, H, D = (q.shape[1], q.shape[2], q.shape[3])

            def step(carry, qkv_t):
                S, z = carry
                qt, kt, vt = qkv_t
                S = S + kt[..., :, None] * vt[..., None, :]
                z = z + kt
                num = jnp.einsum('bhi,bhij->bhj', qt, S)
                den = jnp.sum(qt * z, axis=-1, keepdims=True)
                return ((S, z), num / (den + EPS))
            S0 = jnp.zeros((B, H, D, D), q.dtype)
            z0 = jnp.zeros((B, H, D), q.dtype)
            _, y = jax.lax.scan(step, (S0, z0), (q, k, v))
            return y
        key = jax.random.key(seed)
        k1, k2, k3 = jax.random.split(key, 3)
        B, T, C = (2, 256, 128)
        x = jax.random.normal(k1, (B, T, C), dtype=jnp.float32)
        w_attn = jax.random.normal(k2, (C, 3 * C), dtype=jnp.float32) * 0.02
        w_proj = jax.random.normal(k3, (C, C), dtype=jnp.float32) * 0.02
        return {'x': x, 'w_attn': w_attn, 'w_proj': w_proj}
    _L1_attn_in = _L1_attn_setup()

    def _L1_ffn_setup():
        import jax, jax.numpy as jnp
        import numpy as np
        key = jax.random.key(seed)
        k0, k1, k2, k3 = jax.random.split(key, 4)
        B, S, D, F, E = (8, 256, 128, 256, 8)
        x = jax.random.normal(k0, (B, S, D), dtype=jnp.float32)
        Wg = jax.random.normal(k1, (D, E), dtype=jnp.float32) * 0.02
        W1 = jax.random.normal(k2, (E, D, F), dtype=jnp.float32) * 0.02
        W2 = jax.random.normal(k3, (E, F, D), dtype=jnp.float32) * 0.02
        return {'x': x, 'Wg': Wg, 'W1': W1, 'W2': W2}
    _L1_ffn_in = _L1_ffn_setup()
    _d = {'L0_attn_x': _L0_attn_in['x'], 'L0_attn_Wqkv': _L0_attn_in['Wqkv'], 'L0_attn_Wo': _L0_attn_in['Wo'], 'L0_ffn_W1': _L0_ffn_in['W1'], 'L0_ffn_b1': _L0_ffn_in['b1'], 'L0_ffn_W2': _L0_ffn_in['W2'], 'L0_ffn_b2': _L0_ffn_in['b2'], 'L0_ffn_Wr': _L0_ffn_in['Wr'], 'L0_ffn_br': _L0_ffn_in['br'], 'L1_attn_w_attn': _L1_attn_in['w_attn'], 'L1_attn_w_proj': _L1_attn_in['w_proj'], 'L1_ffn_Wg': _L1_ffn_in['Wg'], 'L1_ffn_W1': _L1_ffn_in['W1'], 'L1_ffn_W2': _L1_ffn_in['W2']}
    _x0 = _d['L0_attn_x']
    _d['L0_attn_x'] = jax.random.normal(jax.random.fold_in(jax.random.key(seed), 1), (16, 256, 128), dtype=_x0.dtype)
    del _x0
    return _d

def reference(L0_attn_x, L0_attn_Wqkv, L0_attn_Wo, L0_ffn_W1, L0_ffn_b1, L0_ffn_W2, L0_ffn_b2, L0_ffn_Wr, L0_ffn_br, L1_attn_w_attn, L1_attn_w_proj, L1_ffn_Wg, L1_ffn_W1, L1_ffn_W2):

    def _L0_attn_ref(x, Wqkv, Wo):
        import jax, jax.numpy as jnp
        import numpy as np
        H = 8
        D = 64
        E = 128

        def sinusoidal_pe(T, d, dtype=jnp.float32):
            pos = jnp.arange(T, dtype=jnp.float32)[:, None]
            div = jnp.exp(jnp.arange(0, d, 2, dtype=jnp.float32) * (-np.log(10000.0) / d))
            ang = pos * div
            pe = jnp.stack([jnp.sin(ang), jnp.cos(ang)], axis=-1).reshape(T, d)
            return pe.astype(dtype)
        B, T, _ = x.shape
        qkv = jnp.einsum('bte,fe->btf', x, Wqkv)
        qkv = qkv.reshape(B, T, H, 3 * D)
        q, k, v = jnp.split(qkv, 3, axis=-1)
        q = q.transpose(0, 2, 1, 3)
        k = k.transpose(0, 2, 1, 3)
        v = v.transpose(0, 2, 1, 3)
        pe = sinusoidal_pe(T, D, q.dtype)
        q = q + pe[None, None]
        k = k + pe[None, None]
        causal = jnp.tril(jnp.ones((T, T), dtype=bool))
        scores = jnp.einsum('bhtd,bhsd->bhts', q, k) / jnp.sqrt(jnp.asarray(D, q.dtype))
        scores = jnp.where(causal[None, None], scores, jnp.asarray(-jnp.inf, q.dtype))
        probs = jax.nn.softmax(scores, axis=-1)
        attn = jnp.einsum('bhts,bhsd->bhtd', probs, v)
        out = attn.transpose(0, 2, 1, 3).reshape(B, T, H * D)
        out = jnp.einsum('btf,ef->bte', out, Wo)
        return out

    def _L0_ffn_ref(x, W1, b1, W2, b2, Wr, br):
        import jax, jax.numpy as jnp
        import numpy as np
        B, S, D, F, E = (4, 256, 128, 512, 8)
        b, s, d = x.shape
        e = Wr.shape[1]
        logits = x @ Wr + br
        idx = jnp.argmax(logits, axis=-1)
        probs = jax.nn.softmax(logits, axis=-1)
        gates = jnp.take_along_axis(probs, idx[..., None], axis=-1)[..., 0]
        xf = x.reshape(-1, d)
        idxf = idx.reshape(-1)
        gf = gates.reshape(-1)
        out = jnp.zeros_like(xf)
        for ei in range(e):
            h = jax.nn.gelu(xf @ W1[ei] + b1[ei], approximate=False)
            y = h @ W2[ei] + b2[ei]
            mask = (idxf == ei).astype(xf.dtype)
            out = out + y * (gf * mask)[:, None]
        return out.reshape(b, s, d)

    def _L1_attn_ref(x, w_attn, w_proj):
        import jax, jax.numpy as jnp
        import numpy as np
        N_HEAD = 16
        EPS = 1e-06

        def _linear_attention(q, k, v):
            B, H, D = (q.shape[1], q.shape[2], q.shape[3])

            def step(carry, qkv_t):
                S, z = carry
                qt, kt, vt = qkv_t
                S = S + kt[..., :, None] * vt[..., None, :]
                z = z + kt
                num = jnp.einsum('bhi,bhij->bhj', qt, S)
                den = jnp.sum(qt * z, axis=-1, keepdims=True)
                return ((S, z), num / (den + EPS))
            S0 = jnp.zeros((B, H, D, D), q.dtype)
            z0 = jnp.zeros((B, H, D), q.dtype)
            _, y = jax.lax.scan(step, (S0, z0), (q, k, v))
            return y
        B, T, C = x.shape
        H = N_HEAD
        D = C // H
        qkv = x @ w_attn
        q, k, v = jnp.split(qkv, 3, axis=-1)

        def to_tbhd(a):
            return a.reshape(B, T, H, D).transpose(1, 0, 2, 3)
        q = jax.nn.elu(to_tbhd(q)) + 1.0
        k = jax.nn.elu(to_tbhd(k)) + 1.0
        v = to_tbhd(v)
        y = _linear_attention(q, k, v)
        y = y.transpose(1, 0, 2, 3).reshape(B, T, C)
        return y @ w_proj

    def _L1_ffn_ref(x, Wg, W1, W2):
        import jax, jax.numpy as jnp
        import numpy as np
        B, S, D = x.shape
        E = Wg.shape[1]
        T = B * S
        cap = max(1, T // E)
        xt = x.reshape(T, D)
        logits = xt @ Wg
        probs = jax.nn.softmax(logits, axis=-1)
        pT = probs.T
        _, top_idx = jax.lax.top_k(pT, cap)
        sel = jnp.zeros((E, T), dtype=bool).at[jnp.arange(E)[:, None], top_idx].set(True)
        masked = jnp.where(sel, pT, -jnp.inf)
        assigned = sel.any(axis=0)
        tok2exp = jnp.where(assigned, jnp.argmax(masked, axis=0), jnp.argmax(pT, axis=0))
        weights = jnp.take_along_axis(probs, tok2exp[:, None], axis=1)[:, 0]
        out = jnp.zeros_like(xt)
        for e in range(E):
            gate = jnp.where(tok2exp == e, weights, 0.0)
            h = jax.nn.gelu(xt @ W1[e], approximate=False) @ W2[e]
            out = out + gate[:, None] * h
        return out.reshape(B, S, D)
    x = L0_attn_x
    x = x + _L0_attn_ref(_layernorm(x, axis=-1), L0_attn_Wqkv, L0_attn_Wo)
    x = x + _L0_ffn_ref(_layernorm(x, axis=-1), L0_ffn_W1, L0_ffn_b1, L0_ffn_W2, L0_ffn_b2, L0_ffn_Wr, L0_ffn_br)
    x = x + _L1_attn_ref(_layernorm(x, axis=-1), L1_attn_w_attn, L1_attn_w_proj)
    x = x + _L1_ffn_ref(_layernorm(x, axis=-1), L1_ffn_Wg, L1_ffn_W1, L1_ffn_W2)
    return x

_drawn_inputs = setup_inputs


def setup_inputs(seed=0):
    import zlib

    import numpy as np

    out = dict(_drawn_inputs(seed))
    spreads = {}
    factors = {'L0_ffn_b1': 8.0,
     'L0_ffn_b2': 8.0,
     'L0_ffn_br': 3.863,
     'L1_attn_w_attn': 5.509,
     'L1_attn_w_proj': 5.375,
     'L1_ffn_Wg': 8.0,
     'L1_ffn_W1': 8.0,
     'L1_ffn_W2': 8.0}
    for name, (base, spread) in spreads.items():
        noise = np.random.default_rng([zlib.crc32(name.encode()), seed]).standard_normal(out[name].shape)
        drawn = base * np.exp(spread * noise) if base else spread * noise
        out[name] = jnp.asarray(drawn.astype(out[name].dtype))
    for name, factor in factors.items():
        out[name] = (out[name] * factor).astype(out[name].dtype)
    return out
```

```python
import numpy as np
import concourse.bass as bass
from concourse import mybir
from contextlib import ExitStack

P = 128
B, T, D = 16, 256, 128
NTOK = B * T
NT = NTOK // P
TB = T // P
H0, DH0 = 8, 64
NPAIR = H0 // 2
VW = DH0 + 1
SCALE0 = DH0 ** -0.5
E = 8
F0, F1 = 512, 256
C0, C1 = F0 // P, F1 // P
H1, DH1 = 16, 8
KV = H1 * DH1 * DH1
CAP = NTOK // E
LN_EPS = 1e-5
LA_EPS = 1e-6
MAXT = NT + E - 1
ROW = D + 4
MEAN, RSTD, GATE, ID = D, D + 1, D + 2, D + 3
W0R = F0 + C0 * D + C0 + D
W1R = F1 + C1 * D
IDENT, UPTO, BEFORE, ONES, MASK, NCONST = 0, P, 2 * P, 3 * P, 4 * P, 5 * P
NEG = -3.0e38
NBITS = 30


def build_model(nc, x_in, consts, pos, sel, wqkv, wo, w0, wr, br, wattn, wproj, wg, w1, bits, out):
    fp32, bf16, i32, u32 = mybir.dt.float32, mybir.dt.bfloat16, mybir.dt.int32, mybir.dt.uint32
    ALU, ACT, AX = mybir.AluOpType, mybir.ActivationFunctionType, mybir.AxisListType

    x_tiles = x_in.rearrange("(t p) d -> p t d", p=P)
    sorted0 = nc.dram_tensor("sorted0", (MAXT * P, ROW), fp32, kind="Internal").ap()
    sorted1 = nc.dram_tensor("sorted1", (MAXT * P, ROW), fp32, kind="Internal").ap()
    x_mid = nc.dram_tensor("x_mid", (NTOK, D), fp32, kind="Internal").ap()
    x_mid_tiles = x_mid.rearrange("(t p) d -> p t d", p=P)

    ctx = ExitStack()
    with ctx:
        def sb(name, shape, dt=fp32):
            return ctx.enter_context(nc.sbuf_tensor(name, shape, dt))

        def sem(name):
            return ctx.enter_context(nc.semaphore(name))

        cf = sb("cf", [P, NCONST])
        cb = sb("cb", [P, NCONST], bf16)
        sel_f = sb("sel_f", [2 * H0, H0 * P])
        sel_b = sb("sel_b", [2 * H0, H0 * P], bf16)
        pos_sb = sb("pos_sb", [P, T])
        wqkv_sb = sb("wqkv_sb", [P, 3 * H0 * DH0])
        wo_sb = sb("wo_sb", [P, NPAIR, D])
        w0_sb = sb("w0_sb", [P, E, W0R])
        wr_sb = sb("wr_sb", [P, E])
        br_sb = sb("br_sb", [P, E])
        wattn_sb = sb("wattn_sb", [P, 3 * D])
        wproj_sb = sb("wproj_sb", [P, D])
        wg_sb = sb("wg_sb", [P, E])
        w1_sb = sb("w1_sb", [P, E, W1R])
        xt = sb("xt", [P, NT, ROW])
        pad = sb("pad", [P, ROW])
        bits_sb = sb("bits_sb", [P, NBITS], i32)
        n_tok = sb("n_tok", [P, 2, TB, D])
        nT = sb("nT", [P, 2, T])
        arena = sb("arena", [P, 2 * (H0 + NPAIR) * T])
        qz = arena[:, 0:2 * H0 * T].rearrange("p (u h t) -> p u h t", u=2, h=H0)
        kp = arena[:, 2 * H0 * T:].rearrange("p (u j t) -> p u j t", u=2, j=NPAIR)
        vv = sb("vv", [P, 2, TB, H0, VW])
        mneg = sb("mneg", [P, 2, TB, H0])
        m16 = sb("m16", [P, 2, TB, 2 * H0], bf16)
        mT = sb("mT", [2 * H0, 2, 3 * P], bf16)
        pT = sb("pT", [P, 4, 3, P])
        rden = sb("rden", [P, TB, 4])
        attn = sb("attn", [P, 2, TB, H0 * DH0])
        aT = sb("aT", [P, TB, NPAIR, P])
        stats = sb("stats", [P, NT, 6])
        mv = sb("mv", [P, NT, 2])
        ve = sb("ve", [P, NT])
        sd = sb("sd", [P, NT])
        rt = sb("rt", [P, NT])
        nrt = sb("nrt", [P, NT])
        rn = sb("rn", [P, 2, 4, D])
        rnT = sb("rnT", [P, 2, 4 * P])
        lg = sb("lg", [P, E, NT])
        ra = sb("ra", [P, E, NT])
        rb = sb("rb", [P, E, NT])
        rc = sb("rc", [P, E, NT])
        rd = sb("rd", [P, E, NT])
        tm = sb("tm", [P, NT])
        tn = sb("tn", [P, NT])
        oh = sb("oh", [P, E, NT])
        ohb = sb("ohb", [P, E, NT], bf16)
        tile0 = sb("tile0", [P, E, NT])
        ewt = sb("ewt", [P, E])
        one8 = sb("one8", [P, E])
        cnt = sb("cnt", [P, E])
        cnti = sb("cnti", [P, E], i32)
        padc = sb("padc", [P, E])
        ends = sb("ends", [P, E])
        base = sb("base", [P, E])
        k128 = sb("k128", [P, MAXT])
        tcmp = sb("tcmp", [P, MAXT, E])
        tef = sb("tef", [P, MAXT])
        te = sb("te", [P, MAXT], i32)
        slots = sb("slots", [P, NT], i32)
        thr = sb("thr", [P, E], i32)
        cand = sb("cand", [P, E], i32)
        keep = sb("keep", [P, E], i32)
        cntb = sb("cntb", [P, E], bf16)
        need = sb("need", [P, E])
        xr = sb("xr", [P, 4, ROW])
        fn = sb("fn", [P, 2, D])
        fnT = sb("fnT", [P, 2, P])
        wb = arena[:, 0:4 * W0R].rearrange("p (n c) -> p n c", n=4)
        hT = sb("hT", [P, 2, F0])
        yb = sb("yb", [P, 2, D])
        yo = sb("yo", [P, 2, D])
        ln = sb("ln", [P, 2, D])
        lnT = sb("lnT", [P, 2, P])
        ex = sb("ex", [P, 2, 2 * D])
        rl = sb("rl", [P, 2, 2 * D])
        ph = sb("ph", [P, 4, 2 * D])
        lv = sb("lv", [P, 2, D])
        kv = arena[:, 0:4 * KV].rearrange("p (n c) -> p n c", n=4)
        mm_ = arena[:, 4 * KV:5 * KV]
        mz = sb("mz", [P, D])
        num = sb("num", [P, D])
        den = sb("den", [P, H1])
        rdn = sb("rdn", [P, H1])
        yl = sb("yl", [P, 2, D])
        ylT = sb("ylT", [P, 2, P])

        bank = [ctx.enter_context(nc.psum_tensor(f"bank{i}", [P, 512], fp32)) for i in range(8)]

        loaded_c = sem("loaded_c")
        loaded_x = sem("loaded_x")
        loaded_a = sem("loaded_a")
        loaded_w = sem("loaded_w")
        padded = sem("padded")
        const_done = sem("const_done")
        pool_const = sem("pool_const")
        pad_ready = sem("pad_ready")
        chain = sem("chain")

        search = sem("search")
        pool_passed, dve_passed = sem("pool_passed"), sem("dve_passed")
        yb_ready, l_red, l_eps, l_rec = sem("yb_ready"), sem("l_red"), sem("l_eps"), sem("l_rec")

        block = ctx.enter_context(nc.Block())

        def wait(eng, s, value):
            if isinstance(value, int) and value <= 0:
                return
            eng.wait_ge(s, value)

        def wait_apart(eng, s, value, passed):
            eng.wait_ge(s, value)
            eng.sem_inc(passed, 1)

        def steady(eng, head, tail, total, body, unroll=2):
            last = head + (total - head - tail) // unroll * unroll
            for k in range(head):
                body(k, k % unroll, k // unroll)
            with eng.Fori(head // unroll, last // unroll) as i:
                for j in range(unroll):
                    body(i * unroll + j, j, i)
            for k in range(last, total):
                body(k, k % unroll, k // unroll)

        def within(k, lo, hi):
            return not isinstance(k, int) or lo <= k < hi

        def bc(ap, shape):
            return ap.to_broadcast(shape)

        ident_f, ident_b = cf[:, IDENT:IDENT + P], cb[:, IDENT:IDENT + P]
        upto_f, ones_f = cf[:, UPTO:UPTO + P], cf[:, ONES:ONES + P]
        before_b, ones_b, mask_b = cb[:, BEFORE:BEFORE + P], cb[:, ONES:ONES + P], cb[:, MASK:MASK + P]

        names = dict(
            var_ready="variances (VectorE)", sd_ready="deviations (ScalarE)", n_stats="mean and rstd",
            n_ready="normalised rows", nt_ps="their transposes in PSUM", nt_sb="and in SBUF",
            g_full="a result in the G banks", g_dve="VectorE read a G bank", g_act="ScalarE read a G bank",
            m_hi="", m_split="", mt_ps="", mt_sb="", e_full="", p_exp="", p_masked="", o_full="", r_done="",
            an_done="", at_full="", at_sb="", proj_full="", res_done="",
        )
        S = {n: sem(n) for n in names}
        var_ready, sd_ready, n_stats = S["var_ready"], S["sd_ready"], S["n_stats"]

        G, Eb, Ob, Tb, Pb = bank[0:2], bank[2:4], bank[4:6], bank[6], bank[7]
        GUSE = 12
        MT_COL = 256
        DVE_USES = [0, 1, 2, 3, 6, 7, 8, 9, 10, 11]
        ACT_USES = [4, 5]

        route_sems = {}
        for r in (0, 1):
            for n in ("rn_ready", "rt_ps", "rt_sb", "lg_done", "lg_free", "exp_in", "exp_out", "oh_ready",
                      "rank_ps", "slot_ready", "scattered", "ge_ready", "cnt_ps",
                      "row_in", "row_used", "w_copied", "fn_ready", "ft_ps", "ft_sb", "h_ps", "h_sb", "y_ps",
                      "y_out", "y_sent"):
                route_sems[n, r] = sem(f"{n}{r}")

        def rs(n, r):
            return route_sems[n, r]

        row_in = [[sem(f"row_in{r}_{n}") for n in range(4)] for r in range(2)]
        y_sent = [[sem(f"y_sent{r}_{n}") for n in range(4)] for r in range(2)]

        def sent(k4):
            return len(range(k4, MAXT, 4))

        l = {n: sem("l_" + n) for n in ("x", "n", "t_ps", "t_sb", "qkv", "exp", "relu", "v", "phi", "kv", "cum",
                                        "mul", "y", "yt_ps", "yt_sb", "pr", "res")}

        @block.sync
        def _(sp):
            sp.dma_start(cf[:, :], consts).then_inc(loaded_c, 16)
            sp.dma_start(xt[:, 0:8, 0:D], x_tiles[:, 0:8, :]).then_inc(loaded_x, 16)
            sp.dma_start(xt[:, 8:NT, 0:D], x_tiles[:, 8:NT, :]).then_inc(loaded_x, 16)
            sp.dma_start(wqkv_sb[:, :], wqkv).then_inc(loaded_a, 16)
            sp.dma_start(pos_sb[:, :], pos).then_inc(loaded_a, 16)
            sp.dma_start(sel_f[:, :], sel).then_inc(loaded_a, 16)
            sp.dma_start(wo_sb[:, :, :], wo).then_inc(loaded_a, 16)
            sp.wait_ge(pad_ready, 1)
            for dst in (sorted0, sorted1):
                with sp.Fori(0, MAXT) as t:
                    sp.dma_start(dst[bass.ts(t, P), :], pad[:, :]).then_inc(padded, 16)
            for dst, src in ((wr_sb, wr), (br_sb, br), (w0_sb, w0), (wattn_sb, wattn), (wproj_sb, wproj),
                             (wg_sb, wg), (w1_sb, w1), (bits_sb, bits)):
                sp.dma_start(dst[:], src).then_inc(loaded_w, 16)

            for r, src in ((0, sorted0), (1, sorted1)):
                sp.wait_ge(rs("scattered", r), 16 * NT)

                def load_rows(k, k4, turn):
                    wait(sp, y_sent[r][k4], 16 * turn)
                    sp.dma_start(xr[:, k4, :], src[bass.ts(k, P), :]).then_inc(row_in[r][k4], 16)
                steady(sp, 4, 1, MAXT, load_rows, 4)
                if r == 0:
                    for k4 in range(4):
                        sp.wait_ge(y_sent[0][k4], 16 * sent(k4))
                    for c in range(4):
                        sp.dma_start(xt[:, 8 * c:8 * c + 8, 0:D], x_mid_tiles[:, 8 * c:8 * c + 8, :]).then_inc(l["x"], 16)
            for k4 in range(4):
                sp.wait_ge(y_sent[1][k4], 16 * sent(k4))

        @block.gpsimd
        def _(pool):
            pool.memset(pad[:, :], 0.0).then_inc(pool_const, 1)
            pool.memset(qz[:, :, :, :], 0.0).then_inc(pool_const, 1)
            pool.memset(vv[:, :, :, :, DH0:VW], 1.0).then_inc(pool_const, 1)
            pool.memset(tile0[:, :, :], 1.0).then_inc(pool_const, 1)
            pool.memset(one8[:, :], 1.0).then_inc(pool_const, 1)
            pool.iota(xt[:, :, ID].bitcast(i32), pattern=[[P, NT]], base=0, channel_multiplier=1).then_inc(pool_const, 1)
            pool.iota(ewt[:, :], pattern=[[-1, E]], base=E, channel_multiplier=0,
                      allow_small_or_imprecise_dtypes=True).then_inc(pool_const, 1)
            pool.iota(k128[:, :], pattern=[[P, MAXT]], base=0, channel_multiplier=0,
                      allow_small_or_imprecise_dtypes=True).then_inc(pool_const, 1)
            pool.wait_ge(pool_const, 8)
            pool.memset(tile0[:, :, 0:1], 0.0).then_inc(pool_const, 1)
            pool.iota(pad[:, ID:ID + 1].bitcast(i32), pattern=[[0, 1]], base=NTOK, channel_multiplier=0).then_inc(pad_ready, 1)

            def mask_probs(b, u, turn):
                for h in range(H0):
                    wait_apart(pool, S["p_exp"], H0 * b + h + 1, pool_passed)
                    blk = pT[:, h % 4, 0:3:2, :]
                    pool.affine_select(out=blk, in_=blk, compare_op=ALU.is_ge, fill=0.0, base=0,
                                       pattern=[[0, 2], [1, P]], channel_multiplier=-1).then_inc(S["p_masked"], 1)
            steady(pool, 2, 2, B, mask_probs)

            pool.wait_ge(padded, 16 * 2 * MAXT)
            for r, dst in ((0, sorted0), (1, sorted1)):
                pool.wait_ge(rs("slot_ready", r), 1)
                for t in range(NT):
                    pool.indirect_dma_start(dst, bass.IndirectOffsetOnAxis(ap=slots[:, t:t + 1].bitcast(u32), axis=0),
                                            xt[:, t, :], None).then_inc(rs("scattered", r), 16)
                target = (x_mid, out)[r]

                def send(k, k4, turn):
                    wait_apart(pool, rs("y_out", r), k + 1, pool_passed)
                    pool.indirect_dma_start(target, bass.IndirectOffsetOnAxis(ap=xr[:, k4, ID:ID + 1].bitcast(u32), axis=0),
                                            yo[:, k4 % 2, :], None, bounds_check=NTOK - 1, oob_is_err=False)\
                        .then_inc(y_sent[r][k4], 16)
                steady(pool, 4, 1, MAXT, send, 4)

        @block.tensor
        def _(pe):
            pe.wait_ge(const_done, 1)
            pe.wait_ge(loaded_a, 16 * 4)
            pe.wait_ge(pool_const, 9)

            def g_wait(b, use):
                prev, pb = (use - 2, b) if use >= 2 else (use - 2 + GUSE, b - 1)
                if isinstance(pb, int) and pb < 0:
                    return
                if prev in DVE_USES:
                    wait(pe, S["g_dve"], len(DVE_USES) * pb + DVE_USES.index(prev) + 1)
                else:
                    wait(pe, S["g_act"], len(ACT_USES) * pb + ACT_USES.index(prev) + 1)

            def transpose_norm(b, u):
                wait(pe, S["n_ready"], b + 1)
                wait(pe, S["nt_sb"], b)
                for tb in range(TB):
                    mm = pe.transpose(Tb[:, tb * P:(tb + 1) * P], n_tok[:, u, tb, :], ident_f)
                mm.then_inc(S["nt_ps"], 1)

            def project_qk(b, u, use):
                if use == 0:
                    wait(pe, S["nt_sb"], b + 1)
                g_wait(b, use)
                pair0, isk = 2 * (use // 2), use % 2
                for j in range(2):
                    col = (isk * NPAIR + pair0 + j) * P
                    mm = pe.matmul(G[use % 2][:, j * T:(j + 1) * T], wqkv_sb[:, col:col + P], nT[:, u, :],
                                   start=True, stop=True)
                mm.then_inc(S["g_full"], 1)

            def project_v(b, u, use):
                g_wait(b, use)
                tb = use - 4
                pe.matmul(G[use % 2][:, :], nT[:, u, tb * P:(tb + 1) * P], wqkv_sb[:, 2 * H0 * DH0:3 * H0 * DH0],
                          start=True, stop=True).then_inc(S["g_full"], 1)

            def score_rows(b, u, use):
                g_wait(b, use)
                half, k = (use - 6) // 3, (use - 6) % 3
                wait(pe, S["g_dve"], len(DVE_USES) * b + 2 * half + 2)
                heads = range(4 * half, 4 * half + 4) if k == 0 else range(4 * half + 2 * (k - 1), 4 * half + 2 * k)
                tb = 0 if k == 0 else 1
                w = P * (tb + 1)
                for n, h in enumerate(heads):
                    o = G[use % 2][:, n * w:(n + 1) * w]
                    pe.matmul(o, qz[:, u, h, tb * P:(tb + 1) * P], kp[:, u, h // 2, 0:w], start=True, stop=False)
                    mm = pe.matmul(o[:, w - P:w], ident_b, mask_b, start=False, stop=True)
                mm.then_inc(S["g_full"], 1)

            def transpose_max(b, u):
                wait(pe, S["m_split"], b + 1)
                wait(pe, S["mt_sb"], b)
                o = Tb[0:2 * H0, MT_COL:MT_COL + 3 * P // 2].bitcast(bf16)
                for n, tb in enumerate((0, 1, 1)):
                    mm = pe.transpose(o[:, n * P:(n + 1) * P], m16[:, u, tb, :], ident_b)
                mm.then_inc(S["mt_ps"], 1)

            def scores(b, u, h):
                if h == 0:
                    wait(pe, S["mt_sb"], b + 1)
                wait(pe, S["p_exp"], H0 * b + h - 1)
                o = Eb[h % 2]
                pe.matmul(o[:, 0:3 * P], sel_b[:, h * P:(h + 1) * P], mT[:, u, :], start=True, stop=False)
                pe.matmul(o[:, 0:T], kp[:, u, h // 2, 0:P], qz[:, u, h, :], start=False, stop=False)
                pe.matmul(o[:, T:3 * P], kp[:, u, h // 2, P:T], qz[:, u, h, P:T], start=False, stop=True)\
                    .then_inc(S["e_full"], 1)

            def values(b, u, h):
                wait(pe, S["p_masked"], H0 * b + h + 1)
                if h % 4 == 0:
                    wait(pe, S["an_done"], 2 * b + h // 4)
                if h == 0:
                    wait(pe, S["g_act"], 2 * b + 2)
                c = (h % 4) * VW
                pe.matmul(Ob[0][:, c:c + VW], pT[:, h % 4, 0, :], vv[:, u, 0, h, :], start=True, stop=True)
                pe.matmul(Ob[1][:, c:c + VW], pT[:, h % 4, 1, :], vv[:, u, 0, h, :], start=True, stop=False)
                pe.matmul(Ob[1][:, c:c + VW], pT[:, h % 4, 2, :], vv[:, u, 1, h, :], start=False, stop=True)\
                    .then_inc(S["o_full"], 1)

            def transpose_attn(b, u, tb):
                wait(pe, S["an_done"], 2 * b + 2)
                if tb == 0:
                    wait(pe, S["res_done"], b)
                else:
                    wait(pe, S["at_sb"], 2 * b + 1)
                for c in range(NPAIR):
                    mm = pe.transpose(Pb[:, c * P:(c + 1) * P], attn[:, u, tb, c * P:(c + 1) * P], ident_f)
                mm.then_inc(S["at_full"], 1)

            def project_out(b, u):
                wait(pe, S["at_sb"], 2 * b + 2)
                for tb in range(TB):
                    for c in range(NPAIR):
                        mm = pe.matmul(Pb[:, tb * P:(tb + 1) * P], aT[:, tb, c, :], wo_sb[:, c, :],
                                       start=(c == 0), stop=(c == NPAIR - 1))
                mm.then_inc(S["proj_full"], 1)

            def front(b, u, n):
                if n == 0:
                    transpose_norm(b, u)
                elif n < 5:
                    project_qk(b, u, n - 1)
                elif n < 7:
                    project_v(b, u, n - 1)
                elif n < 13:
                    score_rows(b, u, n - 1)
                else:
                    transpose_max(b, u)

            SLOT = [[0], [1, 2], [3, 4], [5, 6, 7], [8, 9], [10, 11], [12], [13]]

            for n in range(14):
                front(0, 0, n)

            def attention(b, u, turn):
                for h in range(H0):
                    if within(b, 0, B):
                        scores(b, u, h)
                    if h >= 2:
                        if within(b, 0, B):
                            values(b, u, h - 2)
                    elif within(b, 1, B + 1):
                        values(b - 1, 1 - u, h + 6)
                    if within(b, 0, B - 1):
                        for n in SLOT[h]:
                            front(b + 1, 1 - u, n)
                    if within(b, 1, B + 1):
                        if h == 3:
                            transpose_attn(b - 1, 1 - u, 0)
                        if h == 4:
                            transpose_attn(b - 1, 1 - u, 1)
                        if h == 5:
                            project_out(b - 1, 1 - u)
            steady(pe, 2, 3, B + 1, attention)

            Lb, Rb, Cb = bank[2], bank[3], bank[4]

            def route_logits(r, w):
                def group(g, u):
                    wait(pe, rs("rn_ready", r), g + 1)
                    wait(pe, rs("rt_sb", r), g - 1)
                    for j in range(4):
                        mm = pe.transpose(bank[u][:, j * P:(j + 1) * P], rn[:, u, j, :], ident_f)
                    mm.then_inc(rs("rt_ps", r), 1)

                def logits(g, u):
                    wait(pe, rs("rt_sb", r), g + 1)
                    for j in range(4):
                        mm = pe.matmul(Lb[:, bass.ds((4 * g + j) * E, E)], rnT[:, u, j * P:(j + 1) * P], w[:, :],
                                       start=True, stop=True)
                    mm.then_inc(rs("lg_done", r), 1)
                for g in range(NT // 4 + 1):
                    if g < NT // 4:
                        group(g, g % 2)
                    if g > 0:
                        logits(g - 1, (g - 1) % 2)

            def ranks(r, n):
                wait(pe, rs("oh_ready", r), n)
                pe.matmul(Rb[:, 0:E * NT], before_b, ohb[:, :, :], start=True, stop=True)
                pe.matmul(Rb[:, E * NT:2 * E * NT], ones_b, ohb[:, :, :], start=True, stop=True)\
                    .then_inc(rs("rank_ps", r), 1)

            def experts(r, F):
                C = F // P

                def rows_across(k, u):
                    wait(pe, rs("fn_ready", r), k + 1)
                    wait(pe, rs("ft_sb", r), k - 1)
                    pe.transpose(bank[u][:, 0:P], fn[:, u, :], ident_f).then_inc(rs("ft_ps", r), 1)

                def up(k, u, k4):
                    wait(pe, rs("ft_sb", r), k + 1)
                    wait(pe, rs("w_copied", r), k + 1)
                    wait(pe, rs("h_sb", r), k - 1)
                    for c in range(C):
                        mm = pe.matmul(bank[2 + u][:, c * P:(c + 1) * P], wb[:, k4, c * P:(c + 1) * P], fnT[:, u, :],
                                       start=True, stop=True)
                    mm.then_inc(rs("h_ps", r), 1)

                def down(k, u, k4):
                    wait(pe, rs("h_sb", r), k + 1)
                    wait(pe, rs("y_out", r), k - 1)
                    for c in range(C):
                        mm = pe.matmul(bank[4 + u][:, 0:D], hT[:, u, c * P:(c + 1) * P],
                                       wb[:, k4, F + c * D:F + (c + 1) * D], start=(c == 0), stop=(c == C - 1))
                    mm.then_inc(rs("y_ps", r), 1)

                def step(i, k4, turn):
                    u = k4 % 2
                    if within(i, 1, MAXT + 1):
                        up(i - 1, 1 - u, (k4 - 1) % 4)
                    if within(i, 2, MAXT + 2):
                        down(i - 2, u, (k4 - 2) % 4)
                    if within(i, 0, MAXT):
                        rows_across(i, u)
                steady(pe, 4, 2, MAXT + 2, step, 4)

            pe.wait_ge(loaded_w, 16 * 8)
            route_logits(0, wr_sb)
            ranks(0, 1)
            experts(0, F0)

            def l_turn(k, u):
                wait(pe, l["n"], k + 1)
                wait(pe, l["t_sb"], k)
                pe.transpose(bank[7][:, 0:P], ln[:, u, :], ident_f).then_inc(l["t_ps"], 1)

            def l_qkv(k, u):
                wait(pe, l["t_sb"], k + 1)
                wait(pe, l["v"], k)
                pe.matmul(bank[6][:, 0:3 * D], lnT[:, u, :], wattn_sb[:, :], start=True, stop=True)\
                    .then_inc(l["qkv"], 1)

            def l_cumulate(k, u, k4):
                wait(pe, l["kv"], k + 1)
                wait(pe, l["mul"], k - 1)
                wait(pe, l["res"], k - 1)
                for c in range(2):
                    o = bank[2 + 2 * u + c][:, :]
                    if u == 1:
                        pe.matmul(o, ones_f, kv[:, k4 - 1, c * 512:(c + 1) * 512], start=True, stop=False)
                    pe.matmul(o, upto_f, kv[:, k4, c * 512:(c + 1) * 512], start=(u == 0), stop=True)
                o = bank[u][:, 3 * P:4 * P]
                if u == 1:
                    pe.matmul(o, ones_f, ph[:, k4 - 1, D:2 * D], start=True, stop=False)
                pe.matmul(o, upto_f, ph[:, k4, D:2 * D], start=(u == 0), stop=True).then_inc(l["cum"], 1)

            def l_turn_y(k, u):
                wait(pe, l["y"], k + 1)
                pe.transpose(bank[u][:, P:2 * P], yl[:, u, :], ident_f).then_inc(l["yt_ps"], 1)

            def l_project(k, u):
                wait(pe, l["yt_sb"], k + 1)
                wait(pe, l["res"], k - 1)
                pe.matmul(bank[u][:, 2 * P:3 * P], ylT[:, u, :], wproj_sb[:, :], start=True, stop=True)\
                    .then_inc(l["pr"], 1)

            def linear_attention(i, k4, turn):
                u = k4 % 2
                if within(i, 1, NT + 1):
                    l_qkv(i - 1, 1 - u)
                if within(i, 2, NT + 2):
                    l_cumulate(i - 2, u, (k4 - 2) % 4)
                if within(i, 3, NT + 3):
                    l_turn_y(i - 3, 1 - u)
                    l_project(i - 3, 1 - u)
                if within(i, 0, NT):
                    l_turn(i, u)
            steady(pe, 8, 3, NT + 3, linear_attention, 4)

            route_logits(1, wg_sb)
            with pe.Fori(0, NBITS) as n:
                wait(pe, rs("ge_ready", 1), n + 1)
                pe.matmul(Cb[:, 0:E], ones_b, cntb[:, :], start=True, stop=True).then_inc(rs("cnt_ps", 1), 1)
            for n in range(3):
                ranks(1, n + 1)
            experts(1, F1)

        @block.scalar
        def _(act):
            def deviations(n):
                act.wait_ge(var_ready, n)
                act.activation(sd[:, :], ve[:, :], ACT.Sqrt).then_inc(sd_ready, 1)

            deviations(1)
            act.preload_act_table(ACT.Exp)

            def copy_norm(b, u):
                wait(act, S["nt_ps"], b + 1)
                act.activation(nT[:, u, :], Tb[:, 0:T], ACT.Copy).then_inc(S["nt_sb"], 1)

            def copy_v(b, u):
                for tb in range(TB):
                    wait(act, S["g_full"], GUSE * b + 5 + tb)
                    act.activation(vv[:, u, tb, :, 0:DH0], G[tb][:, :].rearrange("p (h d) -> p h d", h=H0),
                                   ACT.Copy).then_inc(S["g_act"], 1)

            def copy_max(b, u):
                wait(act, S["mt_ps"], b + 1)
                act.activation(mT[:, u, :], Tb[0:2 * H0, MT_COL:MT_COL + 3 * P // 2].bitcast(bf16), ACT.Copy)\
                    .then_inc(S["mt_sb"], 1)

            def exps(b, u, h):
                wait(act, S["e_full"], H0 * b + h + 1)
                wait(act, S["o_full"], H0 * b + h - 3)
                act.activation(pT[:, h % 4, :, :], Eb[h % 2][:, 0:3 * P].rearrange("p (c t) -> p c t", c=3), ACT.Exp,
                               scale=SCALE0).then_inc(S["p_exp"], 1)

            def copy_attn(b, u, tb):
                wait(act, S["at_full"], 2 * b + tb + 1)
                act.activation(aT[:, tb, :, :], Pb[:, :].rearrange("p (c t) -> p c t", c=NPAIR), ACT.Copy)\
                    .then_inc(S["at_sb"], 1)

            act.wait_ge(pool_const, 9)
            copy_norm(0, 0)
            copy_v(0, 0)
            copy_max(0, 0)

            def attention(b, u, turn):
                for h in range(H0):
                    if within(b, 0, B - 1):
                        if h == 0:
                            copy_norm(b + 1, 1 - u)
                        if h == 3:
                            copy_v(b + 1, 1 - u)
                    if within(b, 0, B):
                        exps(b, u, h)
                    if within(b, 1, B + 1) and h in (3, 4):
                        copy_attn(b - 1, 1 - u, h - 3)
                if within(b, 0, B - 1):
                    copy_max(b + 1, 1 - u)
            steady(act, 2, 3, B + 1, attention)

            def route(r):
                for g in range(NT // 4):
                    u = g % 2
                    act.wait_ge(rs("rt_ps", r), g + 1)
                    wait(act, rs("lg_done", r), g - 1)
                    act.activation(rnT[:, u, :], bank[u][:, :], ACT.Copy).then_inc(rs("rt_sb", r), 1)
                act.wait_ge(rs("exp_in", r), 1)
                act.activation(rc[:, :, :], rb[:, :, :], ACT.Exp).then_inc(rs("exp_out", r), 1)

            def experts(r, F):
                C = F // P
                act.preload_act_table(ACT.Gelu)

                def hidden(k, k4, turn):
                    u = k4 % 2
                    wait(act, rs("h_ps", r), k + 1)
                    wait(act, rs("y_ps", r), k - 1)
                    if r == 0:
                        for c in range(C):
                            ins = act.activation(hT[:, u, c * P:(c + 1) * P], bank[2 + u][:, c * P:(c + 1) * P], ACT.Gelu,
                                                 bias=wb[:, k4, F + C * D + c:F + C * D + c + 1])
                    else:
                        ins = act.activation(hT[:, u, 0:F], bank[2 + u][:, 0:F], ACT.Gelu)
                    ins.then_inc(rs("h_sb", r), 1)
                steady(act, 4, 1, MAXT, hidden, 4)

            deviations(2)
            route(0)
            experts(0, F0)

            deviations(3)
            act.preload_act_table(ACT.Exp)

            def linear_attention(i, k4, turn):
                u = k4 % 2
                if within(i, 1, NT + 1):
                    k, v = i - 1, 1 - u
                    qkv = bank[6]
                    wait(act, l["qkv"], k + 1)
                    wait(act, l["phi"], k - 1)
                    act.activation(ex[:, v, :], qkv[:, 0:2 * D], ACT.Exp).then_inc(l["exp"], 1)
                    act.activation(rl[:, v, :], qkv[:, 0:2 * D], ACT.Relu).then_inc(l["relu"], 1)
                    wait(act, l["kv"], k - 1)
                    act.activation(lv[:, v, :], qkv[:, 2 * D:3 * D], ACT.Copy).then_inc(l["v"], 1)
                if within(i, 3, NT + 3):
                    k, v = i - 3, 1 - u
                    wait(act, l["yt_ps"], k + 1)
                    act.activation(ylT[:, v, :], bank[v][:, P:2 * P], ACT.Copy).then_inc(l["yt_sb"], 1)
                if within(i, 0, NT):
                    wait(act, l["t_ps"], i + 1)
                    act.activation(lnT[:, u, :], bank[7][:, 0:P], ACT.Copy).then_inc(l["t_sb"], 1)
            steady(act, 8, 3, NT + 3, linear_attention, 4)

            deviations(4)
            route(1)
            experts(1, F1)

        @block.vector
        def _(dve):
            links = [0]

            def link(ins):
                links[0] += 1
                ins.then_inc(chain, 1)
                dve.wait_ge(chain, links[0])

            def normalise_stats():
                for t in range(NT):
                    last = dve.bn_stats(stats[:, t, :], xt[:, t, 0:D])
                link(last)
                for t in range(NT):
                    last = dve.bn_aggr(mv[:, t, :], stats[:, t, :])
                link(last)
                dve.tensor_copy(xt[:, :, MEAN], mv[:, :, 0])
                dve.tensor_scalar(ve[:, :], mv[:, :, 1], LN_EPS, None, ALU.add).then_inc(var_ready, 1)

            def normalise_rstd(n):
                dve.wait_ge(sd_ready, n)
                link(dve.reciprocal(rt[:, :], sd[:, :]))
                link(dve.tensor_tensor(nrt[:, :], rt[:, :], rt[:, :], ALU.mult))
                link(dve.tensor_tensor(nrt[:, :], nrt[:, :], ve[:, :], ALU.mult))
                link(dve.tensor_scalar(nrt[:, :], nrt[:, :], -0.5, 1.5, ALU.mult, ALU.add))
                link(dve.tensor_tensor(xt[:, :, RSTD], rt[:, :], nrt[:, :], ALU.mult))

            def normalise(dst, row):
                return dve.tensor_scalar(dst, row[:, 0:D], row[:, MEAN:MEAN + 1], row[:, RSTD:RSTD + 1],
                                         ALU.subtract, ALU.mult)

            dve.wait_ge(loaded_c, 16)
            dve.tensor_copy(cb[:, :], cf[:, :])
            dve.wait_ge(loaded_a, 16 * 4)
            dve.tensor_copy(sel_b[:, :], sel_f[:, :]).then_inc(const_done, 1)
            dve.wait_ge(loaded_x, 32)
            normalise_stats()
            normalise_rstd(1)

            dve.wait_ge(pool_const, 9)

            def norm_rows(b, u):
                wait(dve, S["nt_ps"], b - 1)
                for tb in range(TB):
                    ins = normalise(n_tok[:, u, tb, :], xt_row(TB * b + tb))
                ins.then_inc(S["n_ready"], 1)

            def xt_row(t):
                return xt[:, t, :]

            def add_pos(b, u, use):
                wait(dve, S["g_full"], GUSE * b + use + 1)
                ps = G[use % 2][:, :].rearrange("p (j t) -> p j t", j=2)
                pair0 = 2 * (use // 2)
                if use % 2:
                    dve.tensor_tensor(kp[:, u, pair0:pair0 + 2, :], ps, bc(pos_sb[:, None, :], [P, 2, T]), ALU.add)\
                        .then_inc(S["g_dve"], 1)
                else:
                    for half in range(2):
                        rows = slice(64 * half, 64 * half + 64)
                        h0 = 2 * pair0 + half
                        ins = dve.tensor_tensor(qz[rows, u, h0:h0 + 3:2, :], ps[rows], bc(pos_sb[rows, None, :], [64, 2, T]),
                                                ALU.add)
                    ins.then_inc(S["g_dve"], 1)

            def row_max(b, u, use):
                wait(dve, S["g_full"], GUSE * b + use + 1)
                half, k = (use - 6) // 3, (use - 6) % 3
                h0 = 4 * half if k == 0 else 4 * half + 2 * (k - 1)
                nh = 4 if k == 0 else 2
                dve.tensor_reduce(mneg[:, u, int(k > 0), h0:h0 + nh], G[use % 2][:, :].rearrange("p (h s) -> p h s", h=nh),
                                  AX.X, ALU.max, negate=True).then_inc(S["g_dve"], 1)

            def split_max(b, u):
                wait(dve, S["g_dve"], len(DVE_USES) * (b + 1))
                dve.tensor_copy(m16[:, u, :, 0:H0], mneg[:, u, :, :]).then_inc(S["m_hi"], 1)
                wait(dve, S["m_hi"], b + 1)
                dve.tensor_tensor(m16[:, u, :, H0:2 * H0], mneg[:, u, :, :], m16[:, u, :, 0:H0], ALU.subtract)\
                    .then_inc(S["m_split"], 1)

            def divide(b, u, half):
                wait(dve, S["o_full"], H0 * b + 4 * half + 4)
                for tb in range(TB):
                    ps = Ob[tb][:, 0:4 * VW].rearrange("p (h d) -> p h d", h=4)
                    ins = dve.reciprocal(rden[:, tb, :], ps[:, :, DH0])
                ins.then_inc(S["r_done"], 1)
                wait(dve, S["r_done"], 2 * b + half + 1)
                for tb in range(TB):
                    ps = Ob[tb][:, 0:4 * VW].rearrange("p (h d) -> p h d", h=4)
                    o = attn[:, u, tb, half * 4 * DH0:(half + 1) * 4 * DH0].rearrange("p (h d) -> p h d", h=4)
                    ins = dve.tensor_tensor(o, ps[:, :, 0:DH0], bc(rden[:, tb, :, None], [P, 4, DH0]), ALU.mult)
                ins.then_inc(S["an_done"], 1)

            def residual(b, u):
                wait(dve, S["proj_full"], b + 1)
                rows = xt[:, bass.ds(TB * b, TB), 0:D]
                dve.tensor_tensor(rows, Pb[:, 0:TB * D].rearrange("p (t d) -> p t d", t=TB), rows, ALU.add)\
                    .then_inc(S["res_done"], 1)

            norm_rows(0, 0)
            norm_rows(1, 1)
            for use in range(4):
                add_pos(0, 0, use)
            for use in range(6, 12):
                row_max(0, 0, use)
            split_max(0, 0)

            def attention(b, u, turn):
                more = within(b, 0, B - 1)
                if more:
                    add_pos(b + 1, 1 - u, 0)
                    add_pos(b + 1, 1 - u, 1)
                if within(b, 1, B + 1):
                    divide(b - 1, 1 - u, 1)
                if more:
                    add_pos(b + 1, 1 - u, 2)
                    add_pos(b + 1, 1 - u, 3)
                    for use in (6, 7, 8, 9):
                        row_max(b + 1, 1 - u, use)
                if within(b, 0, B):
                    divide(b, u, 0)
                if more:
                    for use in (10, 11):
                        row_max(b + 1, 1 - u, use)
                    split_max(b + 1, 1 - u)
                if within(b, 1, B + 1):
                    residual(b - 1, 1 - u)
                if within(b, 0, B - 2):
                    norm_rows(b + 2, u)
            steady(dve, 2, 3, B + 1, attention)
            dve.wait_ge(S["res_done"], B)

            Lb, Rb, Cb = bank[2], bank[3], bank[4]
            FULL = [P, E, NT]

            def over_e(a):
                return a.rearrange("p e t -> p t e")

            def per_token(a):
                return bc(a[:, None, :], FULL)

            def per_expert(a):
                return bc(a[:, :, None], FULL)

            def logits(r):
                for g in range(NT // 4):
                    u = g % 2
                    wait(dve, rs("rt_ps", r), g - 1)
                    for j in range(4):
                        ins = normalise(rn[:, u, j, :], xt[:, 4 * g + j, :])
                    ins.then_inc(rs("rn_ready", r), 1)
                dve.wait_ge(rs("lg_done", r), NT // 4)
                ps = Lb[:, 0:NT * E].rearrange("p (t e) -> p e t", e=E)
                if r == 0:
                    link(dve.tensor_tensor(lg[:, :, :], ps, per_expert(br_sb[:, :]), ALU.add))
                else:
                    link(dve.tensor_copy(lg[:, :, :], ps))
                link(dve.tensor_reduce(tm[:, :], over_e(lg[:, :, :]), AX.X, ALU.max))
                dve.tensor_tensor(rb[:, :, :], lg[:, :, :], per_token(tm[:, :]), ALU.subtract).then_inc(rs("exp_in", r), 1)

            def first_equal(values):
                link(dve.tensor_tensor(ra[:, :, :], values, per_token(tm[:, :]), ALU.is_equal))
                link(dve.tensor_tensor(ra[:, :, :], ra[:, :, :], per_expert(ewt[:, :]), ALU.mult))
                link(dve.tensor_reduce(tn[:, :], over_e(ra[:, :, :]), AX.X, ALU.max))
                link(dve.tensor_tensor(oh[:, :, :], ra[:, :, :], per_token(tn[:, :]), ALU.is_equal))

            def flags_ranked(flags, r, n):
                dve.tensor_copy(ohb[:, :, :], flags).then_inc(rs("oh_ready", r), 1)
                dve.wait_ge(rs("rank_ps", r), n)
                tot = Rb[:, E * NT:2 * E * NT].rearrange("p (e t) -> p e t", e=E)
                rank = Rb[:, 0:E * NT].rearrange("p (e t) -> p e t", e=E)
                flat = "p e t -> p (e t)"
                link(dve.tensor_tensor_scan(rb[:, :, :].rearrange(flat), tile0[:, :, :].rearrange(flat),
                                            Rb[:, E * NT:2 * E * NT], 0.0, ALU.mult, ALU.add))
                link(dve.tensor_copy(cnt[:, :], rb[:, :, NT - 1]))
                link(dve.tensor_tensor(rd[:, :, :], rb[:, :, :], tot, ALU.subtract))
                link(dve.tensor_tensor(rd[:, :, :], rd[:, :, :], rank, ALU.add))

            def give_slots(r, n):
                flags_ranked(oh[:, :, :], r, n)
                link(dve.tensor_scalar(cnti[:, :], cnt[:, :], float(P - 1), None, ALU.add))
                link(dve.tensor_scalar(cnti[:, :], cnti[:, :], 7, 7, ALU.arith_shift_right, ALU.arith_shift_left))
                link(dve.tensor_copy(padc[:, :], cnti[:, :]))
                link(dve.tensor_tensor_scan(ends[:, :], one8[:, :], padc[:, :], 0.0, ALU.mult, ALU.add))
                link(dve.tensor_tensor(base[:, :], ends[:, :], padc[:, :], ALU.subtract))
                link(dve.tensor_tensor(rd[:, :, :], rd[:, :, :], per_expert(base[:, :]), ALU.add))
                link(dve.tensor_tensor(rd[:, :, :], rd[:, :, :], oh[:, :, :], ALU.mult))
                link(dve.tensor_reduce(tn[:, :], over_e(rd[:, :, :]), AX.X, ALU.add))
                dve.tensor_copy(slots[:, :], tn[:, :]).then_inc(rs("slot_ready", r), 1)
                link(dve.tensor_tensor(tcmp[:, :, :], bc(ends[:, None, :], [P, MAXT, E]), bc(k128[:, :, None], [P, MAXT, E]),
                                       ALU.is_le))
                link(dve.tensor_reduce(tef[:, :], tcmp[:, :, :], AX.X, ALU.add))
                link(dve.tensor_scalar(te[:, :], tef[:, :], float(E - 1), None, ALU.min))

            def experts(r, F, width, weights):
                C = F // P

                def prepare(k, u, k4, turn):
                    expert = dve.value_load(te[0:1, bass.ds(k, 1)], min_val=0, max_val=E - 1)
                    wait(dve, rs("y_ps", r), k - 3)
                    dve.tensor_copy(wb[:, k4, 0:width], weights[:, bass.ds(expert, 1), :].rearrange("p o c -> p (o c)"))\
                        .then_inc(rs("w_copied", r), 1)
                    wait(dve, row_in[r][k4], 16 * (turn + 1))
                    wait(dve, rs("ft_ps", r), k - 1)
                    normalise(fn[:, u, :], xr[:, k4, :]).then_inc(rs("fn_ready", r), 1)

                def evacuate(k, u):
                    wait(dve, rs("ft_ps", r), k + 1)
                    wait(dve, rs("h_ps", r), k - 1)
                    dve.tensor_copy(fnT[:, u, :], bank[u][:, 0:P]).then_inc(rs("ft_sb", r), 1)

                def finish(k, u, k4, turn):
                    wait(dve, rs("y_ps", r), k + 1)
                    wait(dve, y_sent[r][(k4 - 2) % 4], 16 * (turn + 1 if k4 >= 2 else turn))
                    y = bank[4 + u][:, 0:D]
                    if r == 0:
                        b2 = F + C * D + C
                        dve.tensor_tensor(yb[:, u, :], y, wb[:, k4, b2:b2 + D], ALU.add).then_inc(yb_ready, 1)
                        wait(dve, yb_ready, k + 1)
                        y = yb[:, u, :]
                    dve.scalar_tensor_tensor(out=yo[:, u, :], in0=y, scalar=xr[:, k4, GATE:GATE + 1],
                                             in1=xr[:, k4, 0:D], op0=ALU.mult, op1=ALU.add).then_inc(rs("y_out", r), 1)

                def step(i, k4, turn):
                    u = k4 % 2
                    if within(i, 0, MAXT):
                        prepare(i, u, k4, turn)
                    if within(i, 2, MAXT + 2):
                        finish(i - 2, u, (k4 - 2) % 4, turn if k4 >= 2 else turn - 1)
                    if within(i, 0, MAXT):
                        evacuate(i, u)
                steady(dve, 4, 2, MAXT + 2, step, 4)

            dve.wait_ge(loaded_w, 16 * 8)
            normalise_stats()
            normalise_rstd(2)
            logits(0)
            first_equal(lg[:, :, :])
            dve.wait_ge(rs("exp_out", 0), 1)
            link(dve.tensor_reduce(tn[:, :], over_e(rc[:, :, :]), AX.X, ALU.add))
            link(dve.reciprocal(xt[:, :, GATE], tn[:, :]))
            give_slots(0, 1)
            dve.wait_ge(rs("slot_ready", 0), 1)
            experts(0, F0, W0R, w0_sb)

            dve.wait_ge(l["x"], 16 * 4)
            normalise_stats()
            normalise_rstd(3)

            def l_norm(k, u):
                wait(dve, l["t_ps"], k - 1)
                normalise(ln[:, u, :], xt_row(k)).then_inc(l["n"], 1)

            def l_features(k, u, k4):
                wait(dve, l["relu"], k + 1)
                wait(dve, l["cum"], k - 2)
                dve.scalar_tensor_tensor(out=ph[:, k4, :], in0=ex[:, u, :], scalar=1.0, in1=rl[:, u, :],
                                         op0=ALU.min, op1=ALU.add).then_inc(l["phi"], 1)

            def l_outer(k, u, k4):
                wait(dve, l["phi"], k + 1)
                wait(dve, l["v"], k + 1)
                shape = [P, H1, DH1, DH1]
                kk = ph[:, k4, D:2 * D].rearrange("p (h i) -> p h i", h=H1)
                vk = lv[:, u, :].rearrange("p (h j) -> p h j", h=H1)
                dve.tensor_tensor(kv[:, k4, :].rearrange("p (h i j) -> p h i j", h=H1, i=DH1),
                                  bc(kk[:, :, :, None], shape), bc(vk[:, :, None, :], shape), ALU.mult).then_inc(l["kv"], 1)

            def l_read(k, u, k4):
                wait(dve, l["cum"], k + 1)
                wait(dve, l["y"], k)
                q = ph[:, k4, 0:D].rearrange("p (h i) -> p h i", h=H1)
                for c in range(2):
                    hs = slice(c * H1 // 2, (c + 1) * H1 // 2)
                    shape = [P, H1 // 2, DH1, DH1]
                    state = bank[2 + 2 * u + c][:, :].rearrange("p (h i j) -> p h i j", h=H1 // 2, i=DH1)
                    o = mm_[:, c * 512:(c + 1) * 512].rearrange("p (h j i) -> p h i j", h=H1 // 2, i=DH1)
                    dve.tensor_tensor(o, state, bc(q[:, hs, :, None], shape), ALU.mult)
                dve.tensor_tensor(mz[:, :], bank[u][:, 3 * P:4 * P], ph[:, k4, 0:D], ALU.mult).then_inc(l["mul"], 1)
                wait(dve, l["mul"], k + 1)
                dve.tensor_reduce(den[:, :], mz[:, :].rearrange("p (h i) -> p h i", h=H1), AX.X, ALU.add)
                dve.tensor_reduce(num[:, :], mm_[:, :].rearrange("p (g i) -> p g i", i=DH1), AX.X, ALU.add)\
                    .then_inc(l_red, 1)
                wait(dve, l_red, k + 1)
                dve.tensor_scalar(den[:, :], den[:, :], LA_EPS, None, ALU.add).then_inc(l_eps, 1)
                wait(dve, l_eps, k + 1)
                dve.reciprocal(rdn[:, :], den[:, :]).then_inc(l_rec, 1)
                wait(dve, l_rec, k + 1)
                wait(dve, l["yt_ps"], k - 1)
                dve.tensor_tensor(yl[:, u, :].rearrange("p (h j) -> p h j", h=H1), num[:, :].rearrange("p (h j) -> p h j", h=H1),
                                  bc(rdn[:, :, None], [P, H1, DH1]), ALU.mult).then_inc(l["y"], 1)

            def l_residual(k, u):
                wait(dve, l["pr"], k + 1)
                row = xt_row(k)
                dve.tensor_tensor(row[:, 0:D], bank[u][:, 2 * P:3 * P], row[:, 0:D], ALU.add).then_inc(l["res"], 1)

            def linear_attention(i, k4, turn):
                u = k4 % 2
                if within(i, 0, NT):
                    l_norm(i, u)
                if within(i, 1, NT + 1):
                    l_features(i - 1, 1 - u, (k4 - 1) % 4)
                    l_outer(i - 1, 1 - u, (k4 - 1) % 4)
                if within(i, 2, NT + 2):
                    l_read(i - 2, u, (k4 - 2) % 4)
                if within(i, 3, NT + 3):
                    l_residual(i - 3, 1 - u)
            steady(dve, 8, 3, NT + 3, linear_attention, 4)
            dve.wait_ge(l["res"], NT)

            normalise_stats()
            normalise_rstd(4)
            logits(1)
            dve.wait_ge(rs("exp_out", 1), 1)
            link(dve.tensor_reduce(tn[:, :], over_e(rc[:, :, :]), AX.X, ALU.add))
            link(dve.reciprocal(tm[:, :], tn[:, :]))
            link(dve.tensor_tensor(lg[:, :, :], rc[:, :, :], per_token(tm[:, :]), ALU.mult))
            link(dve.memset(thr[:, :], 0))
            with dve.Fori(0, NBITS) as n:
                def step(ins, j):
                    ins.then_inc(search, 1)
                    dve.wait_ge(search, 5 * n + j)
                step(dve.tensor_tensor(cand[:, :], thr[:, :], bc(bits_sb[:, bass.ds(n, 1)], [P, E]), ALU.bitwise_or), 1)
                step(dve.tensor_tensor(ra[:, :, :], lg[:, :, :], per_expert(cand[:, :].bitcast(fp32)), ALU.is_ge), 2)
                step(dve.tensor_reduce(cnt[:, :], ra[:, :, :], AX.X, ALU.add), 3)
                dve.tensor_copy(cntb[:, :], cnt[:, :]).then_inc(rs("ge_ready", 1), 1)
                dve.wait_ge(rs("cnt_ps", 1), n + 1)
                dve.tensor_scalar(keep[:, :], Cb[:, 0:E], float(CAP), None, ALU.is_ge).then_inc(search, 1)
                wait_apart(dve, search, 5 * n + 4, dve_passed)
                step(dve.copy_predicated(thr[:, :], keep[:, :], cand[:, :]), 5)
            thr_f = per_expert(thr[:, :].bitcast(fp32))
            link(dve.tensor_tensor(rc[:, :, :], lg[:, :, :], thr_f, ALU.is_gt))
            flags_ranked(rc[:, :, :], 1, 1)
            link(dve.tensor_scalar(need[:, :], cnt[:, :], -1.0, float(CAP), ALU.mult, ALU.add))
            link(dve.tensor_tensor(oh[:, :, :], lg[:, :, :], thr_f, ALU.is_equal))
            flags_ranked(oh[:, :, :], 1, 2)
            link(dve.tensor_tensor(rd[:, :, :], rd[:, :, :], per_expert(need[:, :]), ALU.is_lt))
            link(dve.tensor_tensor(rd[:, :, :], rd[:, :, :], oh[:, :, :], ALU.mult))
            link(dve.tensor_tensor(rc[:, :, :], rc[:, :, :], rd[:, :, :], ALU.add))
            link(dve.tensor_reduce(tm[:, :], over_e(rc[:, :, :]), AX.X, ALU.max))
            link(dve.tensor_scalar(tm[:, :], tm[:, :], -1.0, 1.0, ALU.mult, ALU.add))
            link(dve.tensor_tensor(rc[:, :, :], rc[:, :, :], per_token(tm[:, :]), ALU.max))
            link(dve.tensor_tensor(ra[:, :, :], lg[:, :, :], rc[:, :, :], ALU.mult))
            link(dve.scalar_tensor_tensor(out=rb[:, :, :], in0=rc[:, :, :], scalar=-1.0, in1=ra[:, :, :],
                                          op0=ALU.add, op1=ALU.add))
            link(dve.tensor_reduce(tm[:, :], over_e(rb[:, :, :]), AX.X, ALU.max))
            link(dve.tensor_copy(xt[:, :, GATE], tm[:, :]))
            first_equal(rb[:, :, :])
            give_slots(1, 3)
            dve.wait_ge(rs("slot_ready", 1), 1)
            experts(1, F1, W1R, w1_sb)


def _constants():
    f = np.float32
    i, j = np.arange(P)[:, None], np.arange(P)[None, :]
    mats = [i == j, i <= j, i < j, np.ones((P, P)), np.where(j > i, NEG, 0.0)]
    consts = np.concatenate([np.asarray(m, f) for m in mats], axis=1)
    pos = np.arange(T, dtype=f)[:, None]
    div = np.exp(np.arange(0, DH0, 2, dtype=f) * f(-np.log(10000.0) / DH0))
    ang = pos * div
    pe = np.stack([np.sin(ang), np.cos(ang)], axis=-1).reshape(T, DH0).T
    pos2 = np.concatenate([pe, pe], axis=0).astype(f)
    sel = np.zeros((2 * H0, H0, P), f)
    for h in range(H0):
        sel[h, h] = 1
        sel[H0 + h, h] = 1
    return consts, pos2, sel.reshape(2 * H0, H0 * P)


def _layout(a):
    consts, pos, sel = _constants()
    w = np.asarray(a["L0_attn_Wqkv"]).reshape(H0, 3, DH0, D)
    wqkv = np.ascontiguousarray(w.transpose(3, 1, 0, 2).reshape(D, 3 * H0 * DH0))
    wo = np.ascontiguousarray(np.asarray(a["L0_attn_Wo"]).T.reshape(NPAIR, P, D).transpose(1, 0, 2))

    def rows(m, c):
        return np.asarray(m).reshape(E, c, P, D).transpose(2, 0, 1, 3).reshape(P, E, c * D)
    w0 = np.concatenate([
        np.asarray(a["L0_ffn_W1"]).transpose(1, 0, 2),
        rows(a["L0_ffn_W2"], C0),
        np.asarray(a["L0_ffn_b1"]).reshape(E, C0, P).transpose(2, 0, 1),
        np.broadcast_to(np.asarray(a["L0_ffn_b2"])[None], (P, E, D)),
    ], axis=2)
    w1 = np.concatenate([np.asarray(a["L1_ffn_W1"]).transpose(1, 0, 2), rows(a["L1_ffn_W2"], C1)], axis=2)
    return dict(
        x=np.asarray(a["L0_attn_x"]).reshape(NTOK, D), consts=consts, pos=pos, sel=sel, wqkv=wqkv, wo=wo, w0=w0,
        wr=np.asarray(a["L0_ffn_Wr"]), br=np.ascontiguousarray(np.broadcast_to(np.asarray(a["L0_ffn_br"])[None], (P, E))),
        wattn=np.asarray(a["L1_attn_w_attn"]), wproj=np.asarray(a["L1_attn_w_proj"]), wg=np.asarray(a["L1_ffn_Wg"]), w1=w1,
        bits=np.ascontiguousarray(np.broadcast_to((1 << np.arange(NBITS - 1, -1, -1)).astype(np.int32)[None], (P, NBITS))))


def kernel(**inputs):
    import concourse.bacc as bacc
    from concourse.bass_utils import run_bass_kernel_spmd as run

    nc = bacc.Bacc("TRN2", target_bir_lowering=False, num_devices=1)
    arrays = {f"in_{k}": np.ascontiguousarray(v) for k, v in _layout(inputs).items()}
    args = [nc.dram_tensor(k, v.shape, mybir.dt.from_np(v.dtype), kind="ExternalInput").ap() for k, v in arrays.items()]
    out = nc.dram_tensor("out", (NTOK, D), mybir.dt.float32, kind="ExternalOutput").ap()
    build_model(nc, *args, out)
    r = run(nc, [arrays], core_ids=[0])
    return r.results[0]["out"].reshape(B, T, D)
```

```python
import numpy as np
import concourse.bass as bass
from concourse import mybir
from contextlib import ExitStack

P = 128
B, T, D = 16, 256, 128
NTOK = B * T
NT = NTOK // P
TB = T // P
H0, DH0 = 8, 64
NPAIR = H0 // 2
SCALE0 = DH0 ** -0.5
E = 8
F0, F1 = 512, 256
C0, C1 = F0 // P, F1 // P
H1, DH1 = 16, 8
KV = H1 * DH1 * DH1
CAP = NTOK // E
LN_EPS = 1e-5
LA_EPS = 1e-6
MAXT = NT + E - 1
RING = 6
ROW = D + 4
MEAN, RSTD, GATE, ID = D, D + 1, D + 2, D + 3
W0R = F0 + C0 * D + C0 + D
W1R = F1 + C1 * D
IDENT, UPTO, BEFORE, ONES, MASK, NCONST = 0, P, 2 * P, 3 * P, 4 * P, 5 * P
NEG = -3.0e38
NBITS = 30


def build_model(nc, x_in, consts, pos, wqkv, wo, w0, wr, br, wattn, wproj, wg, w1, bits, out):
    fp32, bf16, i32, u32 = mybir.dt.float32, mybir.dt.bfloat16, mybir.dt.int32, mybir.dt.uint32
    ALU, ACT, AX = mybir.AluOpType, mybir.ActivationFunctionType, mybir.AxisListType

    x_tiles = x_in.rearrange("(t p) d -> p t d", p=P)
    sorted0 = nc.dram_tensor("sorted0", (MAXT * P, ROW), fp32, kind="Internal").ap()
    sorted1 = nc.dram_tensor("sorted1", (MAXT * P, ROW), fp32, kind="Internal").ap()
    x_mid = nc.dram_tensor("x_mid", (NTOK, D), fp32, kind="Internal").ap()
    x_mid_tiles = x_mid.rearrange("(t p) d -> p t d", p=P)

    ctx = ExitStack()
    with ctx:
        def sb(name, shape, dt=fp32):
            return ctx.enter_context(nc.sbuf_tensor(name, shape, dt))

        def sem(name):
            return ctx.enter_context(nc.semaphore(name))

        cf = sb("cf", [P, NCONST])
        cb = sb("cb", [P, NCONST], bf16)
        pos_sb = sb("pos_sb", [P, 2, T])
        wqkv_sb = sb("wqkv_sb", [P, 3 * H0 * DH0])
        wo_sb = sb("wo_sb", [P, NPAIR, D])
        w0_sb = sb("w0_sb", [P, E, W0R])
        wr_sb = sb("wr_sb", [P, E])
        br_sb = sb("br_sb", [P, E])
        wattn_sb = sb("wattn_sb", [P, 3 * D])
        wproj_sb = sb("wproj_sb", [P, D])
        wg_sb = sb("wg_sb", [P, E])
        w1_sb = sb("w1_sb", [P, E, W1R])
        xt = sb("xt", [P, NT, ROW])
        pad = sb("pad", [P, ROW])
        bits_sb = sb("bits_sb", [P, NBITS], i32)
        n_tok = sb("n_tok", [P, 2, TB, D])
        nT = sb("nT", [P, 2, T])
        arena = sb("arena", [P, RING * W0R])
        qz = arena[:, 0:2 * H0 * T].rearrange("p (u h t) -> p u h t", u=2, h=H0)
        kp = arena[:, 2 * H0 * T:2 * (H0 + NPAIR) * T].rearrange("p (u j t) -> p u j t", u=2, j=NPAIR)
        vv = sb("vv", [P, 2, TB, H0 * DH0])
        mneg = sb("mneg", [P, 2, H0, 3])
        pr = sb("pr", [P, 2, 3, P])
        pT = sb("pT", [P, 4, 3, P])
        den = sb("den", [P, 2, TB, H0])
        rden = sb("rden", [P, TB, H0])
        attn = sb("attn", [P, 2, TB, H0 * DH0])
        aT = sb("aT", [P, TB, NPAIR, P])
        stats = sb("stats", [P, NT, 6])
        mv = sb("mv", [P, NT, 2])
        ve = sb("ve", [P, NT])
        sd = sb("sd", [P, NT])
        rt = sb("rt", [P, NT])
        nrt = sb("nrt", [P, NT])
        rn = sb("rn", [P, 2, 4, D])
        rnT = sb("rnT", [P, 2, 4 * P])
        lg = sb("lg", [P, E, NT])
        ra = sb("ra", [P, E, NT])
        rb = sb("rb", [P, E, NT])
        rc = sb("rc", [P, E, NT])
        rd = sb("rd", [P, E, NT])
        tm = sb("tm", [P, NT])
        tn = sb("tn", [P, NT])
        oh = sb("oh", [P, E, NT])
        ohb = sb("ohb", [P, E, NT], bf16)
        tile0 = sb("tile0", [P, E, NT])
        ewt = sb("ewt", [P, E])
        one8 = sb("one8", [P, E])
        cnt = sb("cnt", [P, E])
        cnti = sb("cnti", [P, E], i32)
        padc = sb("padc", [P, E])
        ends = sb("ends", [P, E])
        base = sb("base", [P, E])
        k128 = sb("k128", [P, MAXT])
        tcmp = sb("tcmp", [P, MAXT, E])
        tef = sb("tef", [P, MAXT])
        te = sb("te", [P, MAXT], i32)
        slots = sb("slots", [P, NT], i32)
        thr = sb("thr", [P, E], i32)
        cand = sb("cand", [P, E], i32)
        keep = sb("keep", [P, E], i32)
        cntb = sb("cntb", [P, E], bf16)
        need = sb("need", [P, E])
        xr = sb("xr", [P, RING, ROW])
        fn = sb("fn", [P, 2, D])
        fnT = sb("fnT", [P, 2, P])
        wb = arena[:, :].rearrange("p (n c) -> p n c", n=RING)
        hT = sb("hT", [P, 2, F0])
        yb = sb("yb", [P, 2, D])
        yo = sb("yo", [P, 3, D])
        ln = sb("ln", [P, 2, D])
        lnT = sb("lnT", [P, 2, P])
        ex = sb("ex", [P, 2, 2 * D])
        rl = sb("rl", [P, 2, 2 * D])
        ph = sb("ph", [P, 4, 2 * D])
        lv = sb("lv", [P, 2, D])
        kv = arena[:, 0:4 * KV].rearrange("p (n c) -> p n c", n=4)
        qs = arena[:, 4 * KV:5 * KV + D]
        num = sb("num", [P, D + H1])
        rdn = sb("rdn", [P, H1])
        lden = sb("lden", [P, H1])
        yl = sb("yl", [P, 2, D])
        ylT = sb("ylT", [P, 2, P])

        bank = [ctx.enter_context(nc.psum_tensor(f"bank{i}", [P, 512], fp32)) for i in range(8)]

        loaded_c = sem("loaded_c")
        loaded_x = sem("loaded_x")
        loaded_a = sem("loaded_a")
        loaded_w = sem("loaded_w")
        padded = sem("padded")
        const_done = sem("const_done")
        pool_const = sem("pool_const")
        pad_ready = sem("pad_ready")
        chain = sem("chain")

        search = sem("search")
        pool_passed, dve_passed = sem("pool_passed"), sem("dve_passed")
        yb_ready, l_red, l_eps, l_rec = sem("yb_ready"), sem("l_red"), sem("l_eps"), sem("l_rec")

        block = ctx.enter_context(nc.Block())

        def wait(eng, s, value):
            if isinstance(value, int) and value <= 0:
                return
            eng.wait_ge(s, value)

        def wait_apart(eng, s, value, passed):
            eng.wait_ge(s, value)
            eng.sem_inc(passed, 1)

        def steady(eng, head, tail, total, body, unroll=2):
            last = head + (total - head - tail) // unroll * unroll
            for k in range(head):
                body(k, k % unroll, k // unroll)
            with eng.Fori(head // unroll, last // unroll) as i:
                for j in range(unroll):
                    body(i * unroll + j, j, i)
            for k in range(last, total):
                body(k, k % unroll, k // unroll)

        def within(k, lo, hi):
            return not isinstance(k, int) or lo <= k < hi

        def bc(ap, shape):
            return ap.to_broadcast(shape)

        ident_f, ident_b = cf[:, IDENT:IDENT + P], cb[:, IDENT:IDENT + P]
        upto_f, ones_f = cf[:, UPTO:UPTO + P], cf[:, ONES:ONES + P]
        before_b, ones_b, mask_b = cb[:, BEFORE:BEFORE + P], cb[:, ONES:ONES + P], cb[:, MASK:MASK + P]

        names = dict(
            var_ready="variances (VectorE)", sd_ready="deviations (ScalarE)", n_stats="mean and rstd",
            n_ready="normalised rows", nt_ps="their transposes in PSUM", nt_sb="and in SBUF",
            g_full="a result in the G banks", g_dve="VectorE read a G bank", g_act="ScalarE read a G bank",
            s_full="scores in PSUM", max_red="", max_done="", p_exp="probabilities", pt_ps="", pt_sb="",
            o_full="", r_done="", an_done="", at_ps="", at_sb="", proj_full="", res_done="",
        )
        S = {n: sem(n) for n in names}
        var_ready, sd_ready, n_stats = S["var_ready"], S["sd_ready"], S["n_stats"]

        G, Sb, Ob, PTb, Mb = bank[0:2], bank[2:4], bank[4:6], bank[6], bank[7]
        route_sems = {}
        for r in (0, 1):
            for n in ("rn_ready", "rt_ps", "rt_sb", "lg_done", "lg_free", "exp_in", "exp_out", "oh_ready",
                      "rank_ps", "slot_ready", "scattered", "ge_ready", "cnt_ps",
                      "row_in", "row_used", "w_copied", "fn_ready", "ft_ps", "ft_sb", "h_ps", "h_sb", "y_ps",
                      "y_out", "y_sent"):
                route_sems[n, r] = sem(f"{n}{r}")

        def rs(n, r):
            return route_sems[n, r]

        row_in = [[sem(f"row_in{r}_{n}") for n in range(RING)] for r in range(2)]
        y_sent = [[sem(f"y_sent{r}_{n}") for n in range(RING)] for r in range(2)]

        def sent(n):
            return len(range(n, MAXT, RING))

        l = {n: sem("l_" + n) for n in ("x", "n", "t_ps", "t_sb", "qkv", "exp", "relu", "v", "phi", "kv", "cum",
                                        "mul", "y", "yt_ps", "yt_sb", "pr", "res")}

        @block.sync
        def _(sp):
            sp.dma_start(cf[:, :], consts).then_inc(loaded_c, 16)
            sp.dma_start(xt[:, 0:8, 0:D], x_tiles[:, 0:8, :]).then_inc(loaded_x, 16)
            sp.dma_start(xt[:, 8:NT, 0:D], x_tiles[:, 8:NT, :]).then_inc(loaded_x, 16)
            sp.dma_start(wqkv_sb[:, :], wqkv).then_inc(loaded_a, 16)
            sp.dma_start(pos_sb[:, :, :], pos).then_inc(loaded_a, 16)
            sp.dma_start(wo_sb[:, :, :], wo).then_inc(loaded_a, 16)
            sp.wait_ge(pad_ready, 1)
            for dst in (sorted0, sorted1):
                with sp.Fori(0, MAXT) as t:
                    sp.dma_start(dst[bass.ts(t, P), :], pad[:, :]).then_inc(padded, 16)
            for dst, src in ((wr_sb, wr), (br_sb, br), (w0_sb, w0), (wattn_sb, wattn), (wproj_sb, wproj),
                             (wg_sb, wg), (w1_sb, w1), (bits_sb, bits)):
                sp.dma_start(dst[:], src).then_inc(loaded_w, 16)

            for r, src in ((0, sorted0), (1, sorted1)):
                sp.wait_ge(rs("scattered", r), 16 * NT)

                def load_rows(k, n, turn):
                    wait(sp, y_sent[r][n], 16 * turn)
                    sp.dma_start(xr[:, n, :], src[bass.ts(k, P), :]).then_inc(row_in[r][n], 16)
                steady(sp, RING, 1, MAXT, load_rows, RING)
                if r == 0:
                    for n in range(RING):
                        sp.wait_ge(y_sent[0][n], 16 * sent(n))
                    for c in range(4):
                        sp.dma_start(xt[:, 8 * c:8 * c + 8, 0:D], x_mid_tiles[:, 8 * c:8 * c + 8, :]).then_inc(l["x"], 16)
            for n in range(RING):
                sp.wait_ge(y_sent[1][n], 16 * sent(n))

        @block.gpsimd
        def _(pool):
            pool.memset(pad[:, :], 0.0).then_inc(pool_const, 1)
            pool.memset(qz[:, :, :, :], 0.0).then_inc(pool_const, 1)
            pool.memset(tile0[:, :, :], 1.0).then_inc(pool_const, 1)
            pool.memset(one8[:, :], 1.0).then_inc(pool_const, 1)
            pool.iota(xt[:, :, ID].bitcast(i32), pattern=[[P, NT]], base=0, channel_multiplier=1).then_inc(pool_const, 1)
            pool.iota(ewt[:, :], pattern=[[-1, E]], base=E, channel_multiplier=0,
                      allow_small_or_imprecise_dtypes=True).then_inc(pool_const, 1)
            pool.iota(k128[:, :], pattern=[[P, MAXT]], base=0, channel_multiplier=0,
                      allow_small_or_imprecise_dtypes=True).then_inc(pool_const, 1)
            pool.wait_ge(pool_const, 7)
            pool.memset(tile0[:, :, 0:1], 0.0).then_inc(pool_const, 1)
            pool.iota(pad[:, ID:ID + 1].bitcast(i32), pattern=[[0, 1]], base=NTOK, channel_multiplier=0).then_inc(pad_ready, 1)

            pool.wait_ge(padded, 16 * 2 * MAXT)
            for r, dst in ((0, sorted0), (1, sorted1)):
                pool.wait_ge(rs("slot_ready", r), 1)
                for t in range(NT):
                    pool.indirect_dma_start(dst, bass.IndirectOffsetOnAxis(ap=slots[:, t:t + 1].bitcast(u32), axis=0),
                                            xt[:, t, :], None).then_inc(rs("scattered", r), 16)
                target = (x_mid, out)[r]

                def send(k, n, turn):
                    wait_apart(pool, rs("y_out", r), k + 1, pool_passed)
                    pool.indirect_dma_start(target, bass.IndirectOffsetOnAxis(ap=xr[:, n, ID:ID + 1].bitcast(u32), axis=0),
                                            yo[:, n % 3, :], None, bounds_check=NTOK - 1, oob_is_err=False)\
                        .then_inc(y_sent[r][n], 16)
                steady(pool, RING, 1, MAXT, send, RING)

        @block.tensor
        def _(pe):
            pe.wait_ge(const_done, 1)
            pe.wait_ge(loaded_a, 16 * 3)
            pe.wait_ge(pool_const, 8)

            def g_wait(b, use):
                prev, pb = (use - 2, b) if use >= 2 else (use + 4, b - 1)
                if isinstance(pb, int) and pb < 0:
                    return
                if prev < 4:
                    wait(pe, S["g_dve"], 4 * pb + prev + 1)
                else:
                    wait(pe, S["g_act"], 2 * pb + prev - 3)

            def transpose_norm(b, u):
                wait(pe, S["n_ready"], b + 1)
                wait(pe, S["res_done"], b - 2)
                for tb in range(TB):
                    mm = pe.transpose(Mb[:, tb * P:(tb + 1) * P], n_tok[:, u, tb, :], ident_f)
                mm.then_inc(S["nt_ps"], 1)

            def project_qk(b, u, use):
                if use == 0:
                    wait(pe, S["nt_sb"], b + 1)
                g_wait(b, use)
                pair0, isk = 2 * (use // 2), use % 2
                for j in range(2):
                    col = (isk * NPAIR + pair0 + j) * P
                    mm = pe.matmul(G[use % 2][:, j * T:(j + 1) * T], wqkv_sb[:, col:col + P], nT[:, u, :],
                                   start=True, stop=True)
                mm.then_inc(S["g_full"], 1)

            def project_v(b, u, use):
                g_wait(b, use)
                tb = use - 4
                pe.matmul(G[use % 2][:, :], nT[:, u, tb * P:(tb + 1) * P], wqkv_sb[:, 2 * H0 * DH0:3 * H0 * DH0],
                          start=True, stop=True).then_inc(S["g_full"], 1)

            def scores(b, u, h):
                if h == 0:
                    wait(pe, S["g_dve"], 4 * b + 4)
                wait(pe, S["p_exp"], H0 * b + h - 1)
                for tb in range(TB):
                    o = Sb[h % 2][:, tb * P:(2 * tb + 1) * P]
                    pe.matmul(o, qz[:, u, h, tb * P:(tb + 1) * P], kp[:, u, h // 2, 0:(tb + 1) * P],
                              start=True, stop=False)
                    mm = pe.matmul(o[:, tb * P:(tb + 1) * P], ident_b, mask_b, start=False, stop=True)
                mm.then_inc(S["s_full"], 1)

            def transpose_probs(b, h):
                wait(pe, S["p_exp"], H0 * b + h + 1)
                wait(pe, S["pt_sb"], H0 * b + h)
                for n in range(3):
                    mm = pe.transpose(PTb[:, n * P:(n + 1) * P], pr[:, h % 2, n, :], ident_f)
                mm.then_inc(S["pt_ps"], 1)

            def values(b, u, h):
                wait(pe, S["pt_sb"], H0 * b + h + 1)
                if h == 0:
                    wait(pe, S["g_act"], 2 * b + 2)
                    wait(pe, S["an_done"], b)
                c = slice(h * DH0, (h + 1) * DH0)
                p3 = (u * H0 + h) % 4
                pe.matmul(Ob[0][:, c], pT[:, p3, 0, :], vv[:, u, 0, c], start=True, stop=True)
                pe.matmul(Ob[1][:, c], pT[:, p3, 1, :], vv[:, u, 0, c], start=True, stop=False)
                pe.matmul(Ob[1][:, c], pT[:, p3, 2, :], vv[:, u, 1, c], start=False, stop=True)\
                    .then_inc(S["o_full"], 1)

            def transpose_attn(b, u, tb):
                wait(pe, S["an_done"], b + 1)
                if tb == 0:
                    wait(pe, S["nt_sb"], min(b + 3, B) if isinstance(b, int) else b + 3)
                else:
                    wait(pe, S["at_sb"], 2 * b + 1)
                for c in range(NPAIR):
                    mm = pe.transpose(Mb[:, c * P:(c + 1) * P], attn[:, u, tb, c * P:(c + 1) * P], ident_f)
                mm.then_inc(S["at_ps"], 1)

            def project_out(b, u):
                wait(pe, S["at_sb"], 2 * b + 2)
                for tb in range(TB):
                    for c in range(NPAIR):
                        mm = pe.matmul(Mb[:, tb * P:(tb + 1) * P], aT[:, tb, c, :], wo_sb[:, c, :],
                                       start=(c == 0), stop=(c == NPAIR - 1))
                mm.then_inc(S["proj_full"], 1)

            def front(b, u, n):
                if n == 0:
                    transpose_norm(b, u)
                elif n < 5:
                    project_qk(b, u, n - 1)
                else:
                    project_v(b, u, n - 1)

            for n in range(7):
                front(0, 0, n)

            def attention(b, u, turn):
                for h in range(H0):
                    if within(b, 0, B):
                        scores(b, u, h)
                    if h >= 2:
                        if within(b, 0, B):
                            values(b, u, h - 2)
                    elif within(b, 1, B + 1):
                        values(b - 1, 1 - u, h + 6)
                    if h >= 1:
                        if within(b, 0, B):
                            transpose_probs(b, h - 1)
                    elif within(b, 1, B + 1):
                        transpose_probs(b - 1, 7)
                    if within(b, 0, B - 1) and h < 7:
                        front(b + 1, 1 - u, h)
                    if within(b, 1, B + 1):
                        if h == 3:
                            transpose_attn(b - 1, 1 - u, 0)
                        if h == 4:
                            transpose_attn(b - 1, 1 - u, 1)
                        if h == 6:
                            project_out(b - 1, 1 - u)
            steady(pe, 2, 3, B + 1, attention)

            Lb, Rb, Cb = bank[2], bank[3], bank[4]

            def route_logits(r, w):
                def group(g, u):
                    wait(pe, rs("rn_ready", r), g + 1)
                    wait(pe, rs("rt_sb", r), g - 1)
                    for j in range(4):
                        mm = pe.transpose(bank[u][:, j * P:(j + 1) * P], rn[:, u, j, :], ident_f)
                    mm.then_inc(rs("rt_ps", r), 1)

                def logits(g, u):
                    wait(pe, rs("rt_sb", r), g + 1)
                    for j in range(4):
                        mm = pe.matmul(Lb[:, bass.ds((4 * g + j) * E, E)], rnT[:, u, j * P:(j + 1) * P], w[:, :],
                                       start=True, stop=True)
                    mm.then_inc(rs("lg_done", r), 1)
                for g in range(NT // 4 + 1):
                    if g < NT // 4:
                        group(g, g % 2)
                    if g > 0:
                        logits(g - 1, (g - 1) % 2)

            def ranks(r, n):
                wait(pe, rs("oh_ready", r), n)
                pe.matmul(Rb[:, 0:E * NT], before_b, ohb[:, :, :], start=True, stop=True)
                pe.matmul(Rb[:, E * NT:2 * E * NT], ones_b, ohb[:, :, :], start=True, stop=True)\
                    .then_inc(rs("rank_ps", r), 1)

            def experts(r, F):
                C = F // P

                def rows_across(k, n):
                    wait(pe, rs("fn_ready", r), k + 1)
                    wait(pe, rs("ft_sb", r), k - 1)
                    pe.transpose(bank[n % 2][:, 0:P], fn[:, n % 2, :], ident_f).then_inc(rs("ft_ps", r), 1)

                def up(k, n):
                    wait(pe, rs("ft_sb", r), k + 1)
                    wait(pe, rs("w_copied", r), k + 1)
                    wait(pe, rs("h_sb", r), k - 1)
                    for c in range(C):
                        mm = pe.matmul(bank[2 + n % 2][:, c * P:(c + 1) * P], wb[:, n, c * P:(c + 1) * P],
                                       fnT[:, n % 2, :], start=True, stop=True)
                    mm.then_inc(rs("h_ps", r), 1)

                def down(k, n):
                    wait(pe, rs("h_sb", r), k + 1)
                    wait(pe, rs("y_out", r), k - 1)
                    for c in range(C):
                        mm = pe.matmul(bank[4 + n % 2][:, 0:D], hT[:, n % 2, c * P:(c + 1) * P],
                                       wb[:, n, F + c * D:F + (c + 1) * D], start=(c == 0), stop=(c == C - 1))
                    mm.then_inc(rs("y_ps", r), 1)

                def step(i, n, turn):
                    if within(i, 1, MAXT + 1):
                        rows_across(i - 1, (n - 1) % RING)
                    if within(i, 2, MAXT + 2):
                        up(i - 2, (n - 2) % RING)
                    if within(i, 3, MAXT + 3):
                        down(i - 3, (n - 3) % RING)
                steady(pe, RING, 4, MAXT + 4, step, RING)

            pe.wait_ge(loaded_w, 16 * 8)
            route_logits(0, wr_sb)
            ranks(0, 1)
            experts(0, F0)

            def l_turn(k, u):
                wait(pe, l["n"], k + 1)
                wait(pe, l["yt_sb"], k - 4)
                pe.transpose(bank[7][:, 0:P], ln[:, u, :], ident_f).then_inc(l["t_ps"], 1)

            def l_qkv(k, u):
                wait(pe, l["t_sb"], k + 1)
                wait(pe, l["v"], k)
                pe.matmul(bank[6][:, 0:3 * D], lnT[:, u, :], wattn_sb[:, :], start=True, stop=True)\
                    .then_inc(l["qkv"], 1)

            def l_cumulate(k, u, k4):
                wait(pe, l["kv"], k + 1)
                wait(pe, l["mul"], k - 1)
                for c in range(2):
                    o = bank[2 + 2 * u + c][:, :]
                    if u == 1:
                        pe.matmul(o, ones_f, kv[:, k4 - 1, c * 512:(c + 1) * 512], start=True, stop=False)
                    pe.matmul(o, upto_f, kv[:, k4, c * 512:(c + 1) * 512], start=(u == 0), stop=True)

            def l_cumulate_k(k, u, k4):
                wait(pe, l["res"], k - 3)
                wait(pe, l["mul"], k - 1)
                o = bank[u][:, 0:P]
                if u == 1:
                    pe.matmul(o, ones_f, ph[:, k4 - 1, D:2 * D], start=True, stop=False)
                pe.matmul(o, upto_f, ph[:, k4, D:2 * D], start=(u == 0), stop=True).then_inc(l["cum"], 1)

            def l_turn_y(k, u):
                wait(pe, l["y"], k + 1)
                pe.transpose(bank[7][:, P:2 * P], yl[:, u, :], ident_f).then_inc(l["yt_ps"], 1)

            def l_project(k, u):
                wait(pe, l["yt_sb"], k + 1)
                wait(pe, l["res"], k - 1)
                pe.matmul(bank[u][:, P:2 * P], ylT[:, u, :], wproj_sb[:, :], start=True, stop=True)\
                    .then_inc(l["pr"], 1)

            def linear_attention(i, k4, turn):
                u = k4 % 2
                if within(i, 1, NT + 1):
                    wait(pe, l["t_sb"], i)
                if within(i, 5, NT + 5):
                    l_turn_y(i - 5, 1 - u)
                if within(i, 1, NT + 1):
                    l_qkv(i - 1, 1 - u)
                if within(i, 3, NT + 3):
                    l_cumulate(i - 3, 1 - u, (k4 - 3) % 4)
                if within(i, 0, NT):
                    l_turn(i, u)
                if within(i, 5, NT + 5):
                    l_project(i - 5, 1 - u)
                if within(i, 3, NT + 3):
                    l_cumulate_k(i - 3, 1 - u, (k4 - 3) % 4)
            steady(pe, 8, 6, NT + 6, linear_attention, 4)

            route_logits(1, wg_sb)
            with pe.Fori(0, NBITS) as n:
                wait(pe, rs("ge_ready", 1), n + 1)
                pe.matmul(Cb[:, 0:E], ones_b, cntb[:, :], start=True, stop=True).then_inc(rs("cnt_ps", 1), 1)
            for n in range(3):
                ranks(1, n + 1)
            experts(1, F1)

        @block.scalar
        def _(act):
            def deviations(n):
                act.wait_ge(var_ready, n)
                act.activation(sd[:, :], ve[:, :], ACT.Sqrt).then_inc(sd_ready, 1)

            deviations(1)
            act.preload_act_table(ACT.Exp)

            def copy_norm(b, u):
                wait(act, S["nt_ps"], b + 1)
                act.activation(nT[:, u, :], Mb[:, 0:T], ACT.Copy).then_inc(S["nt_sb"], 1)

            def copy_v(b, u, tb):
                wait(act, S["g_full"], 6 * b + 5 + tb)
                act.activation(vv[:, u, tb, :], G[tb][:, :], ACT.Copy).then_inc(S["g_act"], 1)

            def exps(b, u, h):
                wait(act, S["max_done"], H0 * b + h + 1)
                wait(act, S["pt_ps"], H0 * b + h - 1)
                act.activation(pr[:, h % 2, 0, :], Sb[h % 2][:, 0:P], ACT.Exp, bias=mneg[:, u, h, 0:1],
                               accum_out=den[:, u, 0, h:h + 1])
                act.activation(pr[:, h % 2, 1:3, :], Sb[h % 2][:, P:3 * P].rearrange("p (n t) -> p n t", n=2), ACT.Exp,
                               bias=mneg[:, u, h, 1:2], accum_out=den[:, u, 1, h:h + 1]).then_inc(S["p_exp"], 1)

            def copy_probs(b, u, h):
                wait(act, S["pt_ps"], H0 * b + h + 1)
                wait(act, S["o_full"], H0 * b + h - 3)
                act.activation(pT[:, h % 4, :, :], PTb[:, 0:3 * P].rearrange("p (n t) -> p n t", n=3), ACT.Copy)\
                    .then_inc(S["pt_sb"], 1)

            def copy_attn(b, u, tb):
                wait(act, S["at_ps"], 2 * b + tb + 1)
                act.activation(aT[:, tb, :, :], Mb[:, :].rearrange("p (c t) -> p c t", c=NPAIR), ACT.Copy)\
                    .then_inc(S["at_sb"], 1)

            act.wait_ge(pool_const, 8)
            copy_norm(0, 0)
            copy_v(0, 0, 0)
            copy_v(0, 0, 1)

            def attention(b, u, turn):
                for h in range(H0):
                    if within(b, 0, B):
                        exps(b, u, h)
                    if h >= 1:
                        if within(b, 0, B):
                            copy_probs(b, u, h - 1)
                    elif within(b, 1, B + 1):
                        copy_probs(b - 1, 1 - u, 7)
                    if within(b, 0, B - 1):
                        if h == 0:
                            copy_norm(b + 1, 1 - u)
                        if h == 5:
                            copy_v(b + 1, 1 - u, 0)
                        if h == 6:
                            copy_v(b + 1, 1 - u, 1)
                    if within(b, 1, B + 1) and h in (3, 4):
                        copy_attn(b - 1, 1 - u, h - 3)
            steady(act, 2, 3, B + 1, attention)

            def route(r):
                for g in range(NT // 4):
                    u = g % 2
                    act.wait_ge(rs("rt_ps", r), g + 1)
                    wait(act, rs("lg_done", r), g - 1)
                    act.activation(rnT[:, u, :], bank[u][:, :], ACT.Copy).then_inc(rs("rt_sb", r), 1)
                act.wait_ge(rs("exp_in", r), 1)
                act.activation(rc[:, :, :], rb[:, :, :], ACT.Exp).then_inc(rs("exp_out", r), 1)

            def experts(r, F):
                C = F // P
                act.preload_act_table(ACT.Gelu)

                def hidden(k, n, turn):
                    u = n % 2
                    wait(act, rs("h_ps", r), k + 1)
                    wait(act, rs("y_ps", r), k - 1)
                    if r == 0:
                        for c in range(C):
                            ins = act.activation(hT[:, u, c * P:(c + 1) * P], bank[2 + u][:, c * P:(c + 1) * P], ACT.Gelu,
                                                 bias=wb[:, n, F + C * D + c:F + C * D + c + 1])
                    else:
                        ins = act.activation(hT[:, u, 0:F], bank[2 + u][:, 0:F], ACT.Gelu)
                    ins.then_inc(rs("h_sb", r), 1)
                steady(act, RING, 1, MAXT, hidden, RING)

            deviations(2)
            route(0)
            experts(0, F0)

            deviations(3)
            act.preload_act_table(ACT.Exp)

            def linear_attention(i, k4, turn):
                u = k4 % 2
                if within(i, 5, NT + 5):
                    k, v = i - 5, 1 - u
                    wait(act, l["yt_ps"], k + 1)
                    wait(act, l["pr"], k - 1)
                    act.activation(ylT[:, v, :], bank[7][:, P:2 * P], ACT.Copy).then_inc(l["yt_sb"], 1)
                if within(i, 1, NT + 1):
                    k, v = i - 1, 1 - u
                    qkv = bank[6]
                    wait(act, l["qkv"], k + 1)
                    wait(act, l["phi"], k - 1)
                    act.activation(ex[:, v, :], qkv[:, 0:2 * D], ACT.Exp).then_inc(l["exp"], 1)
                    act.activation(rl[:, v, :], qkv[:, 0:2 * D], ACT.Relu).then_inc(l["relu"], 1)
                    wait(act, l["kv"], k - 1)
                    act.activation(lv[:, v, :], qkv[:, 2 * D:3 * D], ACT.Copy).then_inc(l["v"], 1)
                if within(i, 0, NT):
                    wait(act, l["t_ps"], i + 1)
                    wait(act, l["qkv"], i - 1)
                    act.activation(lnT[:, u, :], bank[7][:, 0:P], ACT.Copy).then_inc(l["t_sb"], 1)
            steady(act, 8, 6, NT + 6, linear_attention, 4)

            deviations(4)
            route(1)
            experts(1, F1)

        @block.vector
        def _(dve):
            links = [0]

            def link(ins):
                links[0] += 1
                ins.then_inc(chain, 1)
                dve.wait_ge(chain, links[0])

            def normalise_stats():
                for t in range(NT):
                    last = dve.bn_stats(stats[:, t, :], xt[:, t, 0:D])
                link(last)
                for t in range(NT):
                    last = dve.bn_aggr(mv[:, t, :], stats[:, t, :])
                link(last)
                dve.tensor_copy(xt[:, :, MEAN], mv[:, :, 0])
                dve.tensor_scalar(ve[:, :], mv[:, :, 1], LN_EPS, None, ALU.add).then_inc(var_ready, 1)

            def normalise_rstd(n):
                dve.wait_ge(sd_ready, n)
                link(dve.reciprocal(rt[:, :], sd[:, :]))
                link(dve.tensor_tensor(nrt[:, :], rt[:, :], rt[:, :], ALU.mult))
                link(dve.tensor_tensor(nrt[:, :], nrt[:, :], ve[:, :], ALU.mult))
                link(dve.tensor_scalar(nrt[:, :], nrt[:, :], -0.5, 1.5, ALU.mult, ALU.add))
                link(dve.tensor_tensor(xt[:, :, RSTD], rt[:, :], nrt[:, :], ALU.mult))

            def normalise(dst, row):
                return dve.tensor_scalar(dst, row[:, 0:D], row[:, MEAN:MEAN + 1], row[:, RSTD:RSTD + 1],
                                         ALU.subtract, ALU.mult)

            dve.wait_ge(loaded_c, 16)
            dve.tensor_copy(cb[:, :], cf[:, :]).then_inc(const_done, 1)
            dve.wait_ge(loaded_a, 16 * 3)
            dve.wait_ge(loaded_x, 32)
            normalise_stats()
            normalise_rstd(1)

            dve.wait_ge(pool_const, 8)

            def norm_rows(b, u):
                wait(dve, S["nt_ps"], b - 1)
                for tb in range(TB):
                    ins = normalise(n_tok[:, u, tb, :], xt_row(TB * b + tb))
                ins.then_inc(S["n_ready"], 1)

            def xt_row(t):
                return xt[:, t, :]

            def add_pos(b, u, use):
                wait(dve, S["g_full"], 6 * b + use + 1)
                ps = G[use % 2][:, :].rearrange("p (j t) -> p j t", j=2)
                pair0 = 2 * (use // 2)
                if use % 2:
                    dve.tensor_tensor(kp[:, u, pair0:pair0 + 2, :], ps, bc(pos_sb[:, 0:1, :], [P, 2, T]), ALU.add)\
                        .then_inc(S["g_dve"], 1)
                else:
                    for half in range(2):
                        rows = slice(64 * half, 64 * half + 64)
                        h0 = 2 * pair0 + half
                        ins = dve.scalar_tensor_tensor(out=qz[rows, u, h0:h0 + 3:2, :], in0=ps[rows], scalar=SCALE0,
                                                       in1=bc(pos_sb[rows, 1:2, :], [64, 2, T]), op0=ALU.mult, op1=ALU.add)
                    ins.then_inc(S["g_dve"], 1)

            def row_max(b, u, h):
                wait(dve, S["s_full"], H0 * b + h + 1)
                dve.tensor_reduce(mneg[:, u, h, :], Sb[h % 2][:, 0:3 * P].rearrange("p (n s) -> p n s", n=3),
                                  AX.X, ALU.max, negate=True).then_inc(S["max_red"], 1)
                wait(dve, S["max_red"], H0 * b + h + 1)
                dve.tensor_tensor(mneg[:, u, h, 1:2], mneg[:, u, h, 1:2], mneg[:, u, h, 2:3], ALU.min)\
                    .then_inc(S["max_done"], 1)

            def divide(b, u):
                wait(dve, S["o_full"], H0 * (b + 1))
                dve.reciprocal(rden[:, :, :], den[:, u, :, :]).then_inc(S["r_done"], 1)
                wait(dve, S["r_done"], b + 1)
                for tb in range(TB):
                    ins = dve.tensor_tensor(attn[:, u, tb, :].rearrange("p (h d) -> p h d", h=H0),
                                            Ob[tb][:, :].rearrange("p (h d) -> p h d", h=H0),
                                            bc(rden[:, tb, :, None], [P, H0, DH0]), ALU.mult)
                ins.then_inc(S["an_done"], 1)

            def residual(b, u):
                wait(dve, S["proj_full"], b + 1)
                rows = xt[:, bass.ds(TB * b, TB), 0:D]
                dve.tensor_tensor(rows, Mb[:, 0:TB * D].rearrange("p (t d) -> p t d", t=TB), rows, ALU.add)\
                    .then_inc(S["res_done"], 1)

            norm_rows(0, 0)
            norm_rows(1, 1)
            for use in range(4):
                add_pos(0, 0, use)

            def attention(b, u, turn):
                for h in range(H0):
                    if within(b, 0, B):
                        row_max(b, u, h)
                    if h == 1 and within(b, 1, B + 1):
                        divide(b - 1, 1 - u)
                    if 1 <= h <= 4 and within(b, 0, B - 1):
                        add_pos(b + 1, 1 - u, h - 1)
                    if h == 6:
                        if within(b, 0, B - 2):
                            norm_rows(b + 2, u)
                    if h == 7 and within(b, 1, B + 1):
                        residual(b - 1, 1 - u)
            steady(dve, 2, 3, B + 1, attention)
            dve.wait_ge(S["res_done"], B)

            Lb, Rb, Cb = bank[2], bank[3], bank[4]
            FULL = [P, E, NT]

            def over_e(a):
                return a.rearrange("p e t -> p t e")

            def per_token(a):
                return bc(a[:, None, :], FULL)

            def per_expert(a):
                return bc(a[:, :, None], FULL)

            def logits(r):
                for g in range(NT // 4):
                    u = g % 2
                    wait(dve, rs("rt_ps", r), g - 1)
                    for j in range(4):
                        ins = normalise(rn[:, u, j, :], xt[:, 4 * g + j, :])
                    ins.then_inc(rs("rn_ready", r), 1)
                dve.wait_ge(rs("lg_done", r), NT // 4)
                ps = Lb[:, 0:NT * E].rearrange("p (t e) -> p e t", e=E)
                if r == 0:
                    link(dve.tensor_tensor(lg[:, :, :], ps, per_expert(br_sb[:, :]), ALU.add))
                else:
                    link(dve.tensor_copy(lg[:, :, :], ps))
                link(dve.tensor_reduce(tm[:, :], over_e(lg[:, :, :]), AX.X, ALU.max))
                dve.tensor_tensor(rb[:, :, :], lg[:, :, :], per_token(tm[:, :]), ALU.subtract).then_inc(rs("exp_in", r), 1)

            def first_equal(values):
                link(dve.tensor_tensor(ra[:, :, :], values, per_token(tm[:, :]), ALU.is_equal))
                link(dve.tensor_tensor(ra[:, :, :], ra[:, :, :], per_expert(ewt[:, :]), ALU.mult))
                link(dve.tensor_reduce(tn[:, :], over_e(ra[:, :, :]), AX.X, ALU.max))
                link(dve.tensor_tensor(oh[:, :, :], ra[:, :, :], per_token(tn[:, :]), ALU.is_equal))

            def flags_ranked(flags, r, n):
                dve.tensor_copy(ohb[:, :, :], flags).then_inc(rs("oh_ready", r), 1)
                dve.wait_ge(rs("rank_ps", r), n)
                tot = Rb[:, E * NT:2 * E * NT].rearrange("p (e t) -> p e t", e=E)
                rank = Rb[:, 0:E * NT].rearrange("p (e t) -> p e t", e=E)
                flat = "p e t -> p (e t)"
                link(dve.tensor_tensor_scan(rb[:, :, :].rearrange(flat), tile0[:, :, :].rearrange(flat),
                                            Rb[:, E * NT:2 * E * NT], 0.0, ALU.mult, ALU.add))
                link(dve.tensor_copy(cnt[:, :], rb[:, :, NT - 1]))
                link(dve.tensor_tensor(rd[:, :, :], rb[:, :, :], tot, ALU.subtract))
                link(dve.tensor_tensor(rd[:, :, :], rd[:, :, :], rank, ALU.add))

            def give_slots(r, n):
                flags_ranked(oh[:, :, :], r, n)
                link(dve.tensor_scalar(cnti[:, :], cnt[:, :], float(P - 1), None, ALU.add))
                link(dve.tensor_scalar(cnti[:, :], cnti[:, :], 7, 7, ALU.arith_shift_right, ALU.arith_shift_left))
                link(dve.tensor_copy(padc[:, :], cnti[:, :]))
                link(dve.tensor_tensor_scan(ends[:, :], one8[:, :], padc[:, :], 0.0, ALU.mult, ALU.add))
                link(dve.tensor_tensor(base[:, :], ends[:, :], padc[:, :], ALU.subtract))
                link(dve.tensor_tensor(rd[:, :, :], rd[:, :, :], per_expert(base[:, :]), ALU.add))
                link(dve.tensor_tensor(rd[:, :, :], rd[:, :, :], oh[:, :, :], ALU.mult))
                link(dve.tensor_reduce(tn[:, :], over_e(rd[:, :, :]), AX.X, ALU.add))
                dve.tensor_copy(slots[:, :], tn[:, :]).then_inc(rs("slot_ready", r), 1)
                link(dve.tensor_tensor(tcmp[:, :, :], bc(ends[:, None, :], [P, MAXT, E]), bc(k128[:, :, None], [P, MAXT, E]),
                                       ALU.is_le))
                link(dve.tensor_reduce(tef[:, :], tcmp[:, :, :], AX.X, ALU.add))
                link(dve.tensor_scalar(te[:, :], tef[:, :], float(E - 1), None, ALU.min))

            def experts(r, F, width, weights):
                C = F // P

                def prepare(k, n, turn):
                    expert = dve.value_load(te[0:1, bass.ds(k, 1)], min_val=0, max_val=E - 1)
                    wait(dve, row_in[r][n], 16 * (turn + 1))
                    wait(dve, rs("ft_ps", r), k - 1)
                    normalise(fn[:, n % 2, :], xr[:, n, :]).then_inc(rs("fn_ready", r), 1)
                    wait(dve, rs("y_ps", r), k - RING + 1)
                    dve.tensor_copy(wb[:, n, 0:width], weights[:, bass.ds(expert, 1), :].rearrange("p o c -> p (o c)"))\
                        .then_inc(rs("w_copied", r), 1)

                def evacuate(k, n):
                    wait(dve, rs("ft_ps", r), k + 1)
                    wait(dve, rs("h_ps", r), k - 1)
                    dve.tensor_copy(fnT[:, n % 2, :], bank[n % 2][:, 0:P]).then_inc(rs("ft_sb", r), 1)

                def finish(k, n, turn):
                    wait(dve, rs("y_ps", r), k + 1)
                    wait(dve, y_sent[r][(n - 3) % RING], 16 * (turn + 1 if n >= 3 else turn))
                    y = bank[4 + n % 2][:, 0:D]
                    if r == 0:
                        b2 = F + C * D + C
                        dve.tensor_tensor(yb[:, n % 2, :], y, wb[:, n, b2:b2 + D], ALU.add).then_inc(yb_ready, 1)
                        wait(dve, yb_ready, k + 1)
                        y = yb[:, n % 2, :]
                    dve.scalar_tensor_tensor(out=yo[:, n % 3, :], in0=y, scalar=xr[:, n, GATE:GATE + 1],
                                             in1=xr[:, n, 0:D], op0=ALU.mult, op1=ALU.add).then_inc(rs("y_out", r), 1)

                def step(i, n, turn):
                    if within(i, 1, MAXT + 1):
                        evacuate(i - 1, (n - 1) % RING)
                    if within(i, 4, MAXT + 4):
                        finish(i - 4, (n - 4) % RING, turn if n >= 4 else turn - 1)
                    if within(i, 0, MAXT):
                        prepare(i, n, turn)
                steady(dve, RING, 4, MAXT + 4, step, RING)

            dve.wait_ge(loaded_w, 16 * 8)
            normalise_stats()
            normalise_rstd(2)
            logits(0)
            first_equal(lg[:, :, :])
            dve.wait_ge(rs("exp_out", 0), 1)
            link(dve.tensor_reduce(tn[:, :], over_e(rc[:, :, :]), AX.X, ALU.add))
            link(dve.reciprocal(xt[:, :, GATE], tn[:, :]))
            give_slots(0, 1)
            dve.wait_ge(rs("slot_ready", 0), 1)
            experts(0, F0, W0R, w0_sb)

            dve.wait_ge(l["x"], 16 * 4)
            normalise_stats()
            normalise_rstd(3)

            def l_norm(k, u):
                wait(dve, l["t_ps"], k - 1)
                normalise(ln[:, u, :], xt_row(k)).then_inc(l["n"], 1)

            def l_features(k, u, k4):
                wait(dve, l["relu"], k + 1)
                wait(dve, l["cum"], k - 2)
                dve.scalar_tensor_tensor(out=ph[:, k4, :], in0=ex[:, u, :], scalar=1.0, in1=rl[:, u, :],
                                         op0=ALU.min, op1=ALU.add).then_inc(l["phi"], 1)

            def l_outer(k, u, k4):
                wait(dve, l["phi"], k + 1)
                wait(dve, l["v"], k + 1)
                shape = [P, H1, DH1, DH1]
                kk = ph[:, k4, D:2 * D].rearrange("p (h i) -> p h i", h=H1)
                vk = lv[:, u, :].rearrange("p (h j) -> p h j", h=H1)
                dve.tensor_tensor(kv[:, k4, :].rearrange("p (h i j) -> p h i j", h=H1, i=DH1),
                                  bc(kk[:, :, :, None], shape), bc(vk[:, :, None, :], shape), ALU.mult).then_inc(l["kv"], 1)

            def l_query(k, u, k4):
                wait(dve, l["cum"], k + 1)
                wait(dve, l_red, k)
                q = ph[:, k4, 0:D].rearrange("p (h i) -> p h i", h=H1)
                for c in range(2):
                    hs = slice(c * H1 // 2, (c + 1) * H1 // 2)
                    shape = [P, H1 // 2, DH1, DH1]
                    state = bank[2 + 2 * u + c][:, :].rearrange("p (h i j) -> p h i j", h=H1 // 2, i=DH1)
                    o = qs[:, c * 512:(c + 1) * 512].rearrange("p (h j i) -> p h i j", h=H1 // 2, i=DH1)
                    dve.tensor_tensor(o, state, bc(q[:, hs, :, None], shape), ALU.mult)
                dve.tensor_tensor(qs[:, KV:KV + D], bank[u][:, 0:P], ph[:, k4, 0:D], ALU.mult).then_inc(l["mul"], 1)

            def l_sum(k):
                wait(dve, l["mul"], k + 1)
                wait(dve, l["y"], k)
                dve.tensor_reduce(num[:, :], qs[:, :].rearrange("p (g i) -> p g i", i=DH1), AX.X, ALU.add).then_inc(l_red, 1)

            def l_eps_added(k):
                wait(dve, l_red, k + 1)
                dve.tensor_scalar(lden[:, :], num[:, D:D + H1], LA_EPS, None, ALU.add).then_inc(l_eps, 1)

            def l_reciprocal(k):
                wait(dve, l_eps, k + 1)
                dve.reciprocal(rdn[:, :], lden[:, :]).then_inc(l_rec, 1)

            def l_divide(k, u):
                wait(dve, l_rec, k + 1)
                wait(dve, l["yt_ps"], k - 1)
                dve.tensor_tensor(yl[:, u, :].rearrange("p (h j) -> p h j", h=H1),
                                  num[:, 0:D].rearrange("p (h j) -> p h j", h=H1),
                                  bc(rdn[:, :, None], [P, H1, DH1]), ALU.mult).then_inc(l["y"], 1)

            def l_residual(k, u):
                wait(dve, l["pr"], k + 1)
                row = xt_row(k)
                dve.tensor_tensor(row[:, 0:D], bank[u][:, P:2 * P], row[:, 0:D], ALU.add).then_inc(l["res"], 1)

            def linear_attention(i, k4, turn):
                u = k4 % 2
                if within(i, 4, NT + 4):
                    l_query(i - 4, u, k4)
                if within(i, 2, NT + 2):
                    l_features(i - 2, u, (k4 - 2) % 4)
                if within(i, 4, NT + 4):
                    l_sum(i - 4)
                if within(i, 4, NT + 4):
                    l_eps_added(i - 4)
                if within(i, 2, NT + 2):
                    l_outer(i - 2, u, (k4 - 2) % 4)
                if within(i, 0, NT):
                    l_norm(i, u)
                if within(i, 4, NT + 4):
                    l_reciprocal(i - 4)
                if within(i, 6, NT + 6):
                    l_residual(i - 6, u)
                if within(i, 4, NT + 4):
                    l_divide(i - 4, u)
            steady(dve, 8, 6, NT + 6, linear_attention, 4)
            dve.wait_ge(l["res"], NT)

            normalise_stats()
            normalise_rstd(4)
            logits(1)
            dve.wait_ge(rs("exp_out", 1), 1)
            link(dve.tensor_reduce(tn[:, :], over_e(rc[:, :, :]), AX.X, ALU.add))
            link(dve.reciprocal(tm[:, :], tn[:, :]))
            link(dve.tensor_tensor(lg[:, :, :], rc[:, :, :], per_token(tm[:, :]), ALU.mult))
            link(dve.memset(thr[:, :], 0))
            with dve.Fori(0, NBITS) as n:
                def step(ins, j):
                    ins.then_inc(search, 1)
                    dve.wait_ge(search, 5 * n + j)
                step(dve.tensor_tensor(cand[:, :], thr[:, :], bc(bits_sb[:, bass.ds(n, 1)], [P, E]), ALU.bitwise_or), 1)
                step(dve.tensor_tensor(ra[:, :, :], lg[:, :, :], per_expert(cand[:, :].bitcast(fp32)), ALU.is_ge), 2)
                step(dve.tensor_reduce(cnt[:, :], ra[:, :, :], AX.X, ALU.add), 3)
                dve.tensor_copy(cntb[:, :], cnt[:, :]).then_inc(rs("ge_ready", 1), 1)
                dve.wait_ge(rs("cnt_ps", 1), n + 1)
                dve.tensor_scalar(keep[:, :], Cb[:, 0:E], float(CAP), None, ALU.is_ge).then_inc(search, 1)
                wait_apart(dve, search, 5 * n + 4, dve_passed)
                step(dve.copy_predicated(thr[:, :], keep[:, :], cand[:, :]), 5)
            thr_f = per_expert(thr[:, :].bitcast(fp32))
            link(dve.tensor_tensor(rc[:, :, :], lg[:, :, :], thr_f, ALU.is_gt))
            flags_ranked(rc[:, :, :], 1, 1)
            link(dve.tensor_scalar(need[:, :], cnt[:, :], -1.0, float(CAP), ALU.mult, ALU.add))
            link(dve.tensor_tensor(oh[:, :, :], lg[:, :, :], thr_f, ALU.is_equal))
            flags_ranked(oh[:, :, :], 1, 2)
            link(dve.tensor_tensor(rd[:, :, :], rd[:, :, :], per_expert(need[:, :]), ALU.is_lt))
            link(dve.tensor_tensor(rd[:, :, :], rd[:, :, :], oh[:, :, :], ALU.mult))
            link(dve.tensor_tensor(rc[:, :, :], rc[:, :, :], rd[:, :, :], ALU.add))
            link(dve.tensor_reduce(tm[:, :], over_e(rc[:, :, :]), AX.X, ALU.max))
            link(dve.tensor_scalar(tm[:, :], tm[:, :], -1.0, 1.0, ALU.mult, ALU.add))
            link(dve.tensor_tensor(rc[:, :, :], rc[:, :, :], per_token(tm[:, :]), ALU.max))
            link(dve.tensor_tensor(ra[:, :, :], lg[:, :, :], rc[:, :, :], ALU.mult))
            link(dve.scalar_tensor_tensor(out=rb[:, :, :], in0=rc[:, :, :], scalar=-1.0, in1=ra[:, :, :],
                                          op0=ALU.add, op1=ALU.add))
            link(dve.tensor_reduce(tm[:, :], over_e(rb[:, :, :]), AX.X, ALU.max))
            link(dve.tensor_copy(xt[:, :, GATE], tm[:, :]))
            first_equal(rb[:, :, :])
            give_slots(1, 3)
            dve.wait_ge(rs("slot_ready", 1), 1)
            experts(1, F1, W1R, w1_sb)


def _constants():
    f = np.float32
    i, j = np.arange(P)[:, None], np.arange(P)[None, :]
    mats = [i == j, i <= j, i < j, np.ones((P, P)), np.where(j > i, NEG, 0.0)]
    consts = np.concatenate([np.asarray(m, f) for m in mats], axis=1)
    pos = np.arange(T, dtype=f)[:, None]
    div = np.exp(np.arange(0, DH0, 2, dtype=f) * f(-np.log(10000.0) / DH0))
    ang = pos * div
    pe = np.stack([np.sin(ang), np.cos(ang)], axis=-1).reshape(T, DH0).T
    pos2 = np.concatenate([pe, pe], axis=0).astype(f)
    return consts, np.stack([pos2, pos2 * f(SCALE0)], axis=1)


def _layout(a):
    consts, pos = _constants()
    w = np.asarray(a["L0_attn_Wqkv"]).reshape(H0, 3, DH0, D)
    wqkv = np.ascontiguousarray(w.transpose(3, 1, 0, 2).reshape(D, 3 * H0 * DH0))
    wo = np.ascontiguousarray(np.asarray(a["L0_attn_Wo"]).T.reshape(NPAIR, P, D).transpose(1, 0, 2))

    def rows(m, c):
        return np.asarray(m).reshape(E, c, P, D).transpose(2, 0, 1, 3).reshape(P, E, c * D)
    w0 = np.concatenate([
        np.asarray(a["L0_ffn_W1"]).transpose(1, 0, 2),
        rows(a["L0_ffn_W2"], C0),
        np.asarray(a["L0_ffn_b1"]).reshape(E, C0, P).transpose(2, 0, 1),
        np.broadcast_to(np.asarray(a["L0_ffn_b2"])[None], (P, E, D)),
    ], axis=2)
    w1 = np.concatenate([np.asarray(a["L1_ffn_W1"]).transpose(1, 0, 2), rows(a["L1_ffn_W2"], C1)], axis=2)
    return dict(
        x=np.asarray(a["L0_attn_x"]).reshape(NTOK, D), consts=consts, pos=pos, wqkv=wqkv, wo=wo, w0=w0,
        wr=np.asarray(a["L0_ffn_Wr"]), br=np.ascontiguousarray(np.broadcast_to(np.asarray(a["L0_ffn_br"])[None], (P, E))),
        wattn=np.asarray(a["L1_attn_w_attn"]), wproj=np.asarray(a["L1_attn_w_proj"]), wg=np.asarray(a["L1_ffn_Wg"]), w1=w1,
        bits=np.ascontiguousarray(np.broadcast_to((1 << np.arange(NBITS - 1, -1, -1)).astype(np.int32)[None], (P, NBITS))))


def kernel(**inputs):
    import concourse.bacc as bacc
    from concourse.bass_utils import run_bass_kernel_spmd as run

    nc = bacc.Bacc("TRN2", target_bir_lowering=False, num_devices=1)
    arrays = {f"in_{k}": np.ascontiguousarray(v) for k, v in _layout(inputs).items()}
    args = [nc.dram_tensor(k, v.shape, mybir.dt.from_np(v.dtype), kind="ExternalInput").ap() for k, v in arrays.items()]
    out = nc.dram_tensor("out", (NTOK, D), mybir.dt.float32, kind="ExternalOutput").ap()
    build_model(nc, *args, out)
    r = run(nc, [arrays], core_ids=[0])
    return r.results[0]["out"].reshape(B, T, D)
```

```python
import numpy as np
import concourse.bass as bass
from concourse import mybir
from contextlib import ExitStack

P = 128
B, T, D = 16, 256, 128
NTOK = B * T
NT = NTOK // P
TB = T // P
H0, DH0 = 8, 64
NPAIR = H0 // 2
SCALE0 = DH0 ** -0.5
E = 8
F0, F1 = 512, 256
C0, C1 = F0 // P, F1 // P
H1, DH1 = 16, 8
KV = H1 * DH1 * DH1
CAP = NTOK // E
LN_EPS = 1e-5
LA_EPS = 1e-6
CH = 8
NCH = NT // CH
MAXT = NT + E - 1
RING = 6
ROW = D + 4
MEAN, RSTD, GATE, ID = D, D + 1, D + 2, D + 3
W0R = F0 + C0 * D + C0 + D
W1R = F1 + C1 * D
IDENT, UPTO, BEFORE, ONES, SAME, ZERO, MASK, HEADS = [n * P for n in range(8)]
NCONST = HEADS + D + H1
NEG = -3.0e38
ROUNDS = 15


def build_model(nc, x_in, consts, pos, wqkv, wo, w0, wr, br, wattn, wproj, wg, w1, bits, out):
    fp32, bf16, i32, u32 = mybir.dt.float32, mybir.dt.bfloat16, mybir.dt.int32, mybir.dt.uint32
    ALU, ACT, AX = mybir.AluOpType, mybir.ActivationFunctionType, mybir.AxisListType

    x_tiles = x_in.rearrange("(t p) d -> p t d", p=P)
    sorted0 = nc.dram_tensor("sorted0", (MAXT * P, ROW), fp32, kind="Internal").ap()
    sorted1 = nc.dram_tensor("sorted1", (MAXT * P, ROW), fp32, kind="Internal").ap()
    x_mid = nc.dram_tensor("x_mid", (NTOK, D), fp32, kind="Internal").ap()
    x_mid_tiles = x_mid.rearrange("(t p) d -> p t d", p=P)

    ctx = ExitStack()
    with ctx:
        def sb(name, shape, dt=fp32):
            return ctx.enter_context(nc.sbuf_tensor(name, shape, dt))

        def sem(name):
            return ctx.enter_context(nc.semaphore(name))

        cf = sb("cf", [P, NCONST])
        cb = sb("cb", [P, NCONST], bf16)
        pos_sb = sb("pos_sb", [P, 2, T])
        wqkv_sb = sb("wqkv_sb", [P, 3 * H0 * DH0])
        wo_sb = sb("wo_sb", [P, NPAIR, D])
        w0_sb = sb("w0_sb", [P, E, W0R])
        wr_sb = sb("wr_sb", [P, E])
        br_sb = sb("br_sb", [P, E])
        wattn_sb = sb("wattn_sb", [P, 3 * D])
        wproj_sb = sb("wproj_sb", [P, D])
        wg_sb = sb("wg_sb", [P, E])
        w1_sb = sb("w1_sb", [P, E, W1R])
        xt = sb("xt", [P, NT, ROW])
        pad = sb("pad", [P, ROW])
        bits_sb = sb("bits_sb", [P, ROUNDS, 4], i32)
        n_tok = sb("n_tok", [P, 2, TB, D])
        nT = sb("nT", [P, 2, T])
        arena = sb("arena", [P, RING * W0R])
        qz = arena[:, 0:2 * H0 * T].rearrange("p (u h t) -> p u h t", u=2, h=H0)
        kp = arena[:, 2 * H0 * T:2 * (H0 + NPAIR) * T].rearrange("p (u j t) -> p u j t", u=2, j=NPAIR)
        vv = sb("vv", [P, 2, TB, H0 * DH0])
        sneg = sb("sneg", [P, 2, 3, P])
        mneg = sb("mneg", [P, 2, H0, TB])
        pr = sb("pr", [P, 2, 3, P])
        pT = sb("pT", [P, 4, 3, P])
        den = sb("den", [P, 2, TB, H0])
        rden = sb("rden", [P, TB, H0])
        attn = sb("attn", [P, 2, TB, H0 * DH0])
        aT = sb("aT", [P, TB, NPAIR, P])
        stats = sb("stats", [P, NT, 6])
        mv = sb("mv", [P, NT, 2])
        ve = sb("ve", [P, NT])
        shift = sb("shift", [P, NT])
        halves = sb("halves", [P, CH])
        st2 = sb("st2", [P, 2, TB, 6])
        mv2 = sb("mv2", [P, 2, TB, 2])
        ve2 = sb("ve2", [P, 2, TB])
        rn = sb("rn", [P, 2, 4, D])
        rnT = sb("rnT", [P, 2, 4 * P])
        lg = sb("lg", [P, E, NT])
        ra = sb("ra", [P, E, NT])
        rb = sb("rb", [P, E, NT])
        rc = sb("rc", [P, E, NT])
        rd = sb("rd", [P, E, NT])
        tm = sb("tm", [P, NT])
        tn = sb("tn", [P, NT])
        oh = sb("oh", [P, E, NT])
        ohb = sb("ohb", [P, E, NT], bf16)
        tile0 = sb("tile0", [P, E, NT])
        ewt = sb("ewt", [P, E])
        one8 = sb("one8", [P, E])
        cnt = sb("cnt", [P, E])
        cnti = sb("cnti", [P, E], i32)
        padc = sb("padc", [P, E])
        ends = sb("ends", [P, E])
        base = sb("base", [P, E])
        k128 = sb("k128", [P, MAXT])
        tcmp = sb("tcmp", [P, MAXT, E])
        tef = sb("tef", [P, MAXT])
        te = sb("te", [P, MAXT], i32)
        slots = sb("slots", [P, NT], i32)
        by_token = sb("by_token", [P, NT * E])
        lgT = sb("lgT", [P, 2 * P])
        geT = sb("geT", [P, 3, 2 * P])
        flagsT = sb("flagsT", [P, 2, 2 * P])
        thr = sb("thr", [P, 1], i32)
        cand = sb("cand", [P, 4], i32)
        counts = sb("counts", [P, 4], bf16)
        passed = sb("passed", [P, 4])
        need = sb("need", [P, E])
        xr = sb("xr", [P, RING, ROW])
        fn = sb("fn", [P, 2, D])
        fnT = sb("fnT", [P, 2, P])
        wb = arena[:, :].rearrange("p (n c) -> p n c", n=RING)
        hT = sb("hT", [P, 2, F0])
        yb = sb("yb", [P, 2, D])
        yo = sb("yo", [P, 3, D])
        ids = sb("ids", [P, 3, 1], i32)
        ln = sb("ln", [P, 2, D])
        lnT = sb("lnT", [P, 2, P])
        ex = sb("ex", [P, 2, 2 * D])
        rl = sb("rl", [P, 2, 2 * D])
        ph = sb("ph", [P, 4, 2 * D])
        lv = sb("lv", [P, 4, D + H1])
        total = sb("total", [P, D + H1])
        qT = sb("qT", [P, P])
        kv = arena[:, 0:4 * KV].rearrange("p (n c) -> p n c", n=4)
        qs = arena[:, 4 * KV:5 * KV + D]
        num = sb("num", [P, D + H1])
        num2 = sb("num2", [P, D + H1])
        rdn = sb("rdn", [P, H1])
        lden = sb("lden", [P, H1])
        yl = sb("yl", [P, 2, D])
        ylT = sb("ylT", [P, 2, P])
        unused = attn[:, 0, :, :].rearrange("p t c -> p (t c)")[:, 0:5 * D].rearrange("p (n d) -> p n d", n=5)
        lmean = sb("lmean", [P, 4, 1])
        lsq = sb("lsq", [P, 4, 1])
        lve = sb("lve", [P, 4, 1])
        lrstd = sb("lrstd", [P, 4, 1])
        lshift = sb("lshift", [P, 4, 1])

        bank = [ctx.enter_context(nc.psum_tensor(f"bank{i}", [P, 512], fp32)) for i in range(8)]

        loaded_c = sem("loaded_c")
        loaded_x = [sem(f"loaded_x{c}") for c in range(NCH)]
        reloaded = [sem(f"reloaded{c}") for c in range(NCH)]
        stats_done, ve_known, rstd_known = sem("stats_done"), sem("ve_known"), sem("rstd_known")
        multiplied, shift_known = sem("multiplied"), sem("shift_known")
        loaded_a = sem("loaded_a")
        loaded_w = sem("loaded_w")
        padded = sem("padded")
        pool_const = sem("pool_const")
        pad_ready = sem("pad_ready")
        chain = sem("chain")

        search = sem("search")
        pool_passed, dve_passed, act_passed = sem("pool_passed"), sem("dve_passed"), sem("act_passed")
        yb_ready = sem("yb_ready")
        l_red, l_eps, l_rec = sem("l_red"), sem("l_eps"), sem("l_rec")

        block = ctx.enter_context(nc.Block())

        def wait(eng, s, value):
            if isinstance(value, int) and value <= 0:
                return
            eng.wait_ge(s, value)

        def wait_apart(eng, s, value, passed):
            eng.wait_ge(s, value)
            eng.sem_inc(passed, 1)

        def steady(eng, head, tail, total, body, ring=2, turns=1):
            unroll = ring * turns
            last = head + (total - head - tail) // unroll * unroll
            for k in range(head):
                body(k, k % ring, k // ring)
            with eng.Fori(head // unroll, last // unroll) as i:
                for j in range(unroll):
                    body(i * unroll + j, j % ring, i * turns + j // ring)
            for k in range(last, total):
                body(k, k % ring, k // ring)

        def within(k, lo, hi):
            return not isinstance(k, int) or lo <= k < hi

        def bc(ap, shape):
            return ap.to_broadcast(shape)

        ident_f = cf[:, IDENT:IDENT + P]
        upto_f = cf[:, UPTO:UPTO + P]
        heads_f = cf[:, HEADS:HEADS + D + H1]
        same_b = cb[:, SAME:SAME + P]
        before_b, ones_b = cb[:, BEFORE:BEFORE + P], cb[:, ONES:ONES + P]
        masks = [cf[:, MASK:MASK + P], cf[:, ZERO:MASK + P]]

        G, Sb, Ob, PTb, Mb = bank[0:2], bank[2:4], bank[4:6], bank[6], bank[7]

        names = dict(
            n_ready="a sequence's normalised rows in SBUF (VectorE)",
            nt_ps="the first two sequences' rows turned, in PSUM (TensorE)",
            nt_sb="a tile of turned rows in SBUF (ScalarE)",
            g_full="a projection in a G bank (TensorE)",
            g_dve="q or k taken from a G bank (VectorE)",
            g_act="v taken from a G bank (ScalarE)",
            s_full="a head's scores in PSUM (TensorE)",
            max_done="its masked scores in SBUF, with the rows' maxima (VectorE)",
            p_exp="its exponentials and their sums (ScalarE)",
            pt_ps="the exponentials turned, in PSUM (TensorE)",
            pt_sb="and in SBUF (ScalarE)",
            o_full="its output in the O banks (TensorE)",
            r_done="a sequence's 1 / sums (VectorE)",
            an_done="its attention, divided, in SBUF (VectorE)",
            at_ps="a tile of it turned, in PSUM (TensorE)",
            at_sb="and in SBUF (ScalarE)",
            proj_full="the sequence's projection in PSUM (TensorE)",
            res_done="its residual stream updated (VectorE)",
        )
        S = {n: sem(n) for n in names}

        both = ("exp_in", "exp_out",
                "oh_ready", "rank_ps",
                "slot_ready", "scattered",
                "w_copied", "fn_ready",
                "ft_ps", "ft_sb",
                "h_ps", "h_sb",
                "y_ps", "y_out")
        first = ("bn_done", "mv_done",
                 "ve_done", "norm_known",
                 "rn_ready", "rt_ps", "rt_sb",
                 "lg_done", "lg_copied")
        second = ("p_ready", "p_turned",
                  "ge_ready", "cnt_ps",
                  "f_ready", "f_turned")
        route_sems = {(n, r): sem(f"{n}{r}") for r, own in ((0, first), (1, second)) for n in both + own}

        def rs(n, r):
            return route_sems[n, r]

        row_in = [[sem(f"row_in{r}_{n}") for n in range(RING)] for r in range(2)]
        y_sent = [[sem(f"y_sent{r}_{n}") for n in range(RING)] for r in range(2)]

        def sent(n):
            return len(range(n, MAXT, RING))

        l = {n: sem("l_" + n) for n in (
            "n", "t_ps", "t_sb",
            "q_ps", "q_sb",
            "before", "joined",
            "qkv", "relu", "v",
            "phi", "kv", "cum",
            "mul", "y",
            "yt_ps", "yt_sb", "pr", "res",
            "mean", "squares",
            "ve", "rstd", "known",
            "rn", "route_ps", "route_sb")}

        @block.sync
        def _(sp):
            def load_x(c, src, sems):
                sp.dma_start(xt[:, CH * c:CH * (c + 1), 0:D], src[:, CH * c:CH * (c + 1), :]).then_inc(sems[c], 16)
            load_x(0, x_tiles, loaded_x)
            sp.dma_start(cf[:, :], consts).then_inc(loaded_c, 16)
            sp.dma_start(wqkv_sb[:, :], wqkv).then_inc(loaded_a, 16)
            sp.dma_start(pos_sb[:, :, :], pos).then_inc(loaded_a, 16)
            for c in range(1, NCH):
                load_x(c, x_tiles, loaded_x)
            sp.dma_start(wo_sb[:, :, :], wo).then_inc(loaded_w, 16)
            for dst, src in ((wr_sb, wr), (br_sb, br), (w0_sb, w0), (wattn_sb, wattn), (wproj_sb, wproj),
                             (wg_sb, wg), (w1_sb, w1), (bits_sb, bits)):
                sp.dma_start(dst[:], src).then_inc(loaded_w, 16)
            sp.wait_ge(pad_ready, 1)
            for dst in (sorted0, sorted1):
                with sp.Fori(0, MAXT) as t:
                    sp.dma_start(dst[bass.ts(t, P), :], pad[:, :]).then_inc(padded, 16)

            for r, src in ((0, sorted0), (1, sorted1)):
                sp.wait_ge(rs("scattered", r), 16 * NT)

                def load_rows(k, n, turn):
                    wait(sp, rs("y_out", r), k - RING + 1)
                    sp.dma_start(xr[:, n, :], src[bass.ts(k, P), :]).then_inc(row_in[r][n], 16)
                steady(sp, 2 * RING, 1, MAXT, load_rows, RING, 2)
                if r == 0:
                    for n in range(RING):
                        sp.wait_ge(y_sent[0][n], 16 * sent(n))
                    for c in range(NCH):
                        load_x(c, x_mid_tiles, reloaded)
            for n in range(RING):
                sp.wait_ge(y_sent[1][n], 16 * sent(n))

        @block.gpsimd
        def _(pool):
            pool.memset(pad[:, :], 0.0).then_inc(pool_const, 1)
            pool.memset(qz[:, :, :, :], 0.0).then_inc(pool_const, 1)
            pool.memset(tile0[:, :, :], 1.0).then_inc(pool_const, 1)
            pool.memset(one8[:, :], 1.0).then_inc(pool_const, 1)
            pool.memset(halves[:, :], -0.5).then_inc(pool_const, 1)
            pool.memset(lv[:, :, D:D + H1], 1.0).then_inc(pool_const, 1)
            pool.iota(xt[:, :, ID].bitcast(i32), pattern=[[P, NT]], base=0, channel_multiplier=1).then_inc(pool_const, 1)
            pool.iota(ewt[:, :], pattern=[[-1, E]], base=E, channel_multiplier=0,
                      allow_small_or_imprecise_dtypes=True).then_inc(pool_const, 1)
            pool.iota(k128[:, :], pattern=[[P, MAXT]], base=0, channel_multiplier=0,
                      allow_small_or_imprecise_dtypes=True).then_inc(pool_const, 1)
            pool.wait_ge(pool_const, 9)
            pool.memset(tile0[:, :, 0:1], 0.0).then_inc(pool_const, 1)
            pool.iota(pad[:, ID:ID + 1].bitcast(i32), pattern=[[0, 1]], base=NTOK, channel_multiplier=0).then_inc(pad_ready, 1)

            def rstd_chunk(n):
                tiles = slice(CH * (n % NCH), CH * (n % NCH + 1))
                pool.wait_ge(stats_done, n + 1)
                pool.tensor_scalar(ve[:, tiles], mv[:, tiles, 1], LN_EPS, None, ALU.add).then_inc(ve_known, 1)
                pool.tensor_copy(xt[:, tiles, MEAN], mv[:, tiles, 0])
                pool.wait_ge(ve_known, n + 1)
                pool.tensor_tensor(xt[:, tiles, RSTD], ve[:, tiles], halves[:, 0:CH], ALU.pow).then_inc(rstd_known, 1)
                if n >= NCH:
                    pool.wait_ge(rstd_known, n + 1)
                    pool.tensor_tensor(shift[:, tiles], xt[:, tiles, MEAN], xt[:, tiles, RSTD], ALU.mult)\
                        .then_inc(multiplied, 1)
                    pool.wait_ge(multiplied, n - NCH + 1)
                    pool.tensor_scalar(shift[:, tiles], shift[:, tiles], -1.0, None, ALU.mult).then_inc(shift_known, 1)
            for c in range(NCH):
                rstd_chunk(c)

            def rstd(b, u, turn):
                wait_apart(pool, rs("mv_done", 0), b + 1, pool_passed)
                pool.tensor_scalar(ve2[:, u, :], mv2[:, u, :, 1], LN_EPS, None, ALU.add).then_inc(rs("ve_done", 0), 1)
                pool.tensor_copy(xt[:, bass.ds(TB * b, TB), MEAN], mv2[:, u, :, 0])
                wait_apart(pool, rs("ve_done", 0), b + 1, pool_passed)
                pool.tensor_tensor(xt[:, bass.ds(TB * b, TB), RSTD], ve2[:, u, :], halves[:, 0:TB], ALU.pow)\
                    .then_inc(rs("norm_known", 0), 1)
            steady(pool, 2, 1, B, rstd)

            pool.wait_ge(padded, 16 * 2 * MAXT)
            for r, dst in ((0, sorted0), (1, sorted1)):
                pool.wait_ge(rs("slot_ready", r), 1)
                for t in range(NT):
                    pool.indirect_dma_start(dst, bass.IndirectOffsetOnAxis(ap=slots[:, t:t + 1].bitcast(u32), axis=0),
                                            xt[:, t, :], None).then_inc(rs("scattered", r), 16)
                target = (x_mid, out)[r]

                def send(k, n, turn):
                    wait_apart(pool, rs("y_out", r), k + 1, pool_passed)
                    pool.indirect_dma_start(target, bass.IndirectOffsetOnAxis(ap=ids[:, n % 3, :].bitcast(u32), axis=0),
                                            yo[:, n % 3, :], None, bounds_check=NTOK - 1, oob_is_err=False)\
                        .then_inc(y_sent[r][n], 16)
                steady(pool, 2 * RING, 1, MAXT, send, RING, 2)
                if r == 1:
                    break

                rstd_chunk(NCH)

                def l_outer(k, u, k4):
                    wait(pool, l["phi"], k + 1)
                    wait(pool, l["v"], k + 1)
                    shape = [P, H1, DH1, DH1]
                    kk = ph[:, k4, D:2 * D].rearrange("p (h i) -> p h i", h=H1)
                    vk = lv[:, k4, 0:D].rearrange("p (h j) -> p h j", h=H1)
                    pool.tensor_tensor(kv[:, k4, :].rearrange("p (h i j) -> p h i j", h=H1, i=DH1),
                                      bc(kk[:, :, :, None], shape), bc(vk[:, :, None, :], shape), ALU.mult).then_inc(l["kv"], 1)

                def l_statistics(k, k4):
                    wait_apart(pool, l["squares"], k + 1, pool_passed)
                    pool.tensor_scalar(lve[:, k4, :], lsq[:, k4, :], 1.0 / D, LN_EPS, ALU.mult, ALU.add).then_inc(l["ve"], 1)
                    pool.tensor_copy(xt[:, bass.ds(k, 1), MEAN], lmean[:, k4, :])
                    wait(pool, l["ve"], k + 1)
                    pool.tensor_tensor(lrstd[:, k4, :], lve[:, k4, :], halves[:, 0:1], ALU.pow).then_inc(l["rstd"], 1)
                    wait_apart(pool, l["rstd"], k + 1, pool_passed)
                    pool.tensor_copy(xt[:, bass.ds(k, 1), RSTD], lrstd[:, k4, :])
                    pool.tensor_scalar(lshift[:, k4, :], lmean[:, k4, :], lrstd[:, k4, :], -1.0, ALU.mult, ALU.mult)\
                        .then_inc(l["known"], 1)

                def l_step(i, k4, turn):
                    if isinstance(i, int) and 1 <= i < NCH:
                        rstd_chunk(NCH + i)
                    if within(i, 0, NT):
                        l_outer(i, k4 % 2, k4)
                    if within(i, 6, NT + 6):
                        l_statistics(i - 6, (k4 - 6) % 4)
                steady(pool, 8, 6, NT + 6, l_step, 4)


        @block.tensor
        def _(pe):
            pe.wait_ge(loaded_c, 16)
            pe.wait_ge(loaded_a, 16 * 2)
            pe.wait_ge(pool_const, 10)

            def g_wait(b, use):
                prev, pb = (use - 2, b) if use >= 2 else (use + 4, b - 1)
                if isinstance(pb, int) and pb < 0:
                    return
                if prev < 4:
                    wait(pe, S["g_dve"], 4 * pb + prev + 1)
                else:
                    wait(pe, S["g_act"], 2 * pb + prev - 3)

            def turn_norm(b, u, tb):
                wait(pe, S["n_ready"], b + 1)
                wait(pe, S["pt_sb"], H0 * (b - 2) + 4 + tb)
                pe.transpose(PTb[:, 3 * P:4 * P], n_tok[:, u, tb, :], ident_f)

            def project_qk(b, u, use):
                if use == 0:
                    wait(pe, S["nt_sb"], TB * (b + 1))
                g_wait(b, use)
                pair0, isk = 2 * (use // 2), use % 2
                for j in range(2):
                    col = (isk * NPAIR + pair0 + j) * P
                    mm = pe.matmul(G[use % 2][:, j * T:(j + 1) * T], wqkv_sb[:, col:col + P], nT[:, u, :],
                                   start=True, stop=True)
                mm.then_inc(S["g_full"], 1)

            def project_v(b, u, use):
                g_wait(b, use)
                tb = use - 4
                pe.matmul(G[use % 2][:, :], nT[:, u, tb * P:(tb + 1) * P], wqkv_sb[:, 2 * H0 * DH0:3 * H0 * DH0],
                          start=True, stop=True).then_inc(S["g_full"], 1)

            def scores(b, u, h):
                if h == 0:
                    wait(pe, S["g_dve"], 4 * b + 4)
                wait(pe, S["max_done"], H0 * b + h - 1)
                for tb in range(TB):
                    mm = pe.matmul(Sb[h % 2][:, tb * P:(2 * tb + 1) * P], qz[:, u, h, tb * P:(tb + 1) * P],
                                   kp[:, u, h // 2, 0:(tb + 1) * P], start=True, stop=True)
                mm.then_inc(S["s_full"], 1)

            def transpose_probs(b, h):
                wait(pe, S["p_exp"], H0 * b + h + 1)
                wait(pe, S["pt_sb"], H0 * b + h)
                for n in range(3):
                    mm = pe.transpose(PTb[:, n * P:(n + 1) * P], pr[:, h % 2, n, :], ident_f)
                mm.then_inc(S["pt_ps"], 1)

            def turn_route(b, u, tb):
                wait(pe, rs("rn_ready", 0), b + 1)
                if within(b + 3, 0, B):
                    wait(pe, S["pt_sb"], H0 * (b + 3) + tb)
                else:
                    wait(pe, S["pt_sb"], H0 * B)
                    wait(pe, rs("rt_sb", 0), 2 * b + tb)
                mm = pe.transpose(PTb[:, 3 * P:4 * P], rn[:, u, tb, :], ident_f)
                if not within(b + 3, 0, B):
                    mm.then_inc(rs("rt_ps", 0), 1)

            def route_logits_of(b):
                wait(pe, rs("rt_sb", 0), 2 * b + 2)
                for tb in range(TB):
                    mm = pe.matmul(Mb[:, T + tb * E:T + (tb + 1) * E], rnT[:, 0, tb * P:(tb + 1) * P], wr_sb[:, :],
                                   start=True, stop=True)
                if not within(b + 3, 1, B + 1):
                    mm.then_inc(rs("lg_done", 0), 1)

            def values(b, u, h):
                wait(pe, S["pt_sb"], H0 * b + h + 1)
                if h == 0:
                    wait(pe, S["g_act"], 2 * b + 2)
                    wait(pe, S["an_done"], b)
                c = slice(h * DH0, (h + 1) * DH0)
                p3 = (u * H0 + h) % 4
                pe.matmul(Ob[0][:, c], pT[:, p3, 0, :], vv[:, u, 0, c], start=True, stop=True)
                pe.matmul(Ob[1][:, c], pT[:, p3, 1, :], vv[:, u, 0, c], start=True, stop=False)
                pe.matmul(Ob[1][:, c], pT[:, p3, 2, :], vv[:, u, 1, c], start=False, stop=True)\
                    .then_inc(S["o_full"], 1)

            def transpose_attn(b, u, tb):
                wait(pe, S["an_done"], b + 1)
                if tb == 0:
                    wait(pe, S["res_done"], b)
                else:
                    wait(pe, S["at_sb"], 2 * b + 1)
                for c in range(NPAIR):
                    mm = pe.transpose(Mb[:, c * P:(c + 1) * P], attn[:, u, tb, c * P:(c + 1) * P], ident_f)
                mm.then_inc(S["at_ps"], 1)

            def project_out(b, tb):
                wait(pe, S["at_sb"], 2 * b + 2)
                if isinstance(b, int) and b == 0:
                    pe.wait_ge(loaded_w, 16 * 9)
                for c in range(NPAIR):
                    mm = pe.matmul(Mb[:, tb * P:(tb + 1) * P], aT[:, tb, c, :], wo_sb[:, c, :],
                                   start=(c == 0), stop=(c == NPAIR - 1))
                if tb == TB - 1:
                    mm.then_inc(S["proj_full"], 1)

            def front(b, u, n):
                if n < 4:
                    project_qk(b, u, n)
                else:
                    project_v(b, u, n)

            for b in range(2):
                wait(pe, S["n_ready"], b + 1)
                for tb in range(TB):
                    mm = pe.transpose(Mb[:, (TB * b + tb) * P:(TB * b + tb + 1) * P], n_tok[:, b, tb, :], ident_f)
            mm.then_inc(S["nt_ps"], 1)
            for n in range(6):
                front(0, 0, n)

            def attention(b, u, turn):
                for h in range(H0):
                    if within(b, 0, B):
                        scores(b, u, h)
                    if h >= 2:
                        if within(b, 0, B):
                            values(b, u, h - 2)
                    elif within(b, 1, B + 1):
                        values(b - 1, 1 - u, h + 6)
                    if h in (1, 2) and within(b, 3, B + 3):
                        turn_route(b - 3, 1 - u, h - 1)
                    if h in (5, 6) and within(b, 0, B - 2):
                        turn_norm(b + 2, u, h - 5)
                    if h >= 1:
                        if within(b, 0, B):
                            transpose_probs(b, h - 1)
                    elif within(b, 1, B + 1):
                        transpose_probs(b - 1, 7)
                    if within(b, 0, B - 1) and h < 6:
                        front(b + 1, 1 - u, h)
                    if within(b, 1, B + 1):
                        if h == 3:
                            transpose_attn(b - 1, 1 - u, 0)
                        if h == 4:
                            transpose_attn(b - 1, 1 - u, 1)
                        if h == 6 and within(b, 3, B + 3):
                            wait(pe, S["at_sb"], 2 * b)
                            route_logits_of(b - 3)
                        if h >= 6:
                            project_out(b - 1, h - 6)
                    elif h == 6 and within(b, 3, B + 3):
                        wait(pe, S["res_done"], B)
                        wait(pe, rs("lg_copied", 0), b - B - 1)
                        route_logits_of(b - 3)
            steady(pe, 4, 5, B + 3, attention)

            Lb, Rb, Cb = bank[2], bank[3], bank[4]

            def ranks(r, n):
                wait(pe, rs("oh_ready", r), n)
                pe.matmul(Rb[:, 0:E * NT], before_b, ohb[:, :, :], start=True, stop=True)
                pe.matmul(Rb[:, E * NT:2 * E * NT], ones_b, ohb[:, :, :], start=True, stop=True)\
                    .then_inc(rs("rank_ps", r), 1)

            def experts(r, F):
                C = F // P

                def rows_across(k, n):
                    wait(pe, rs("fn_ready", r), k + 1)
                    wait(pe, rs("ft_sb", r), k - 1)
                    pe.transpose(bank[n % 2][:, 0:P], fn[:, n % 2, :], ident_f).then_inc(rs("ft_ps", r), 1)

                def up(k, n):
                    wait(pe, rs("ft_sb", r), k + 1)
                    wait(pe, rs("w_copied", r), k + 1)
                    wait(pe, rs("h_sb", r), k - 1)
                    for c in range(C):
                        mm = pe.matmul(bank[2 + n % 2][:, c * P:(c + 1) * P], wb[:, n, c * P:(c + 1) * P],
                                       fnT[:, n % 2, :], start=True, stop=True)
                    mm.then_inc(rs("h_ps", r), 1)

                def down(k, n):
                    wait(pe, rs("h_sb", r), k + 1)
                    wait(pe, rs("y_out", r), k - 1)
                    for c in range(C):
                        mm = pe.matmul(bank[4 + n % 2][:, 0:D], hT[:, n % 2, c * P:(c + 1) * P],
                                       wb[:, n, F + c * D:F + (c + 1) * D], start=(c == 0), stop=(c == C - 1))
                    mm.then_inc(rs("y_ps", r), 1)

                def step(i, n, turn):
                    if within(i, 1, MAXT + 1):
                        rows_across(i - 1, (n - 1) % RING)
                    if within(i, 2, MAXT + 2):
                        up(i - 2, (n - 2) % RING)
                    if within(i, 3, MAXT + 3):
                        down(i - 3, (n - 3) % RING)
                steady(pe, 2 * RING, 4, MAXT + 4, step, RING, 2)

            ranks(0, 1)
            experts(0, F0)

            def l_turn(k, u):
                wait(pe, l["n"], k + 1)
                wait(pe, l["yt_sb"], k - 4)
                pe.transpose(bank[7][:, 0:P], ln[:, u, :], ident_f).then_inc(l["t_ps"], 1)

            def l_turn_q(k, k4):
                wait(pe, l["phi"], k + 1)
                wait(pe, l["v"], k + 3 if not isinstance(k, int) else min(k + 3, NT))
                pe.transpose(bank[6][:, 3 * D:4 * D], ph[:, k4, 0:D], ident_f).then_inc(l["q_ps"], 1)

            def l_before(k, pair):
                wait(pe, l["q_sb"], pair + 1)
                wait(pe, l["mul"], k + 1)
                wait(pe, l["res"], k - 1)
                pe.matmul(bank[1][:, 2 * P:2 * P + D + H1], qT[:, :], total[:, :], start=True, stop=True)\
                    .then_inc(l["before"], 1)

            def l_qkv(k, u, pair):
                wait(pe, l["t_sb"], k + 1)
                wait(pe, l["v"], k)
                if u == 0:
                    wait(pe, l["q_sb"], pair)
                pe.matmul(bank[6][:, 0:3 * D], lnT[:, u, :], wattn_sb[:, :], start=True, stop=True)\
                    .then_inc(l["qkv"], 1)

            def l_cumulate(k, u, k4, c):
                wait(pe, l["kv"], k + 1)
                wait(pe, l["mul"], k - 1)
                o = bank[2 + 2 * u + c][:, :]
                pe.matmul(o, upto_f, kv[:, k4, c * 512:(c + 1) * 512], start=True, stop=True)

            def l_cumulate_k(k, u, k4):
                wait(pe, l["res"], k - 3)
                wait(pe, l["mul"], k - 1)
                o = bank[u][:, 0:P]
                if u == 0:
                    pe.matmul(bank[u][:, 2 * P:2 * P + D + H1], ph[:, k4, D:2 * D], lv[:, k4, :], start=True, stop=True)
                pe.matmul(o, upto_f, ph[:, k4, D:2 * D], start=True, stop=True).then_inc(l["cum"], 1)

            def l_route(i, u):
                wait(pe, l["yt_sb"], min(i - 4, NT) if isinstance(i, int) else i - 4)
                wait(pe, l["route_sb"], i - 10)
                if within(i, 10, NT + 10):
                    wait(pe, l["rn"], i - 9)
                    mm = pe.transpose(bank[7][:, 2 * P:3 * P], rn[:, u, 0, :], ident_f)
                if within(i, 11, NT + 11):
                    mm = pe.matmul(bank[7][:, 3 * P:3 * P + E], rnT[:, 0, (1 - u) * P:(2 - u) * P], wg_sb[:, :],
                                   start=True, stop=True)
                mm.then_inc(l["route_ps"], 1)

            def l_turn_y(k, u):
                wait(pe, l["y"], k + 1)
                wait(pe, l["t_sb"], min(k + 5, NT) if isinstance(k, int) else k + 5)
                wait(pe, l["route_sb"], k - 5)
                pe.transpose(bank[7][:, P:2 * P], yl[:, u, :], ident_f).then_inc(l["yt_ps"], 1)

            def l_project(k, u):
                wait(pe, l["yt_sb"], k + 1)
                wait(pe, l["res"], k - 1)
                pe.matmul(bank[u][:, P:2 * P], ylT[:, u, :], wproj_sb[:, :], start=True, stop=True)\
                    .then_inc(l["pr"], 1)

            def linear_attention(i, k4, turn):
                u = k4 % 2
                pairs = i // 2 if isinstance(i, int) else 2 * turn + k4 // 2
                if within(i, 1, NT + 1):
                    l_qkv(i - 1, 1 - u, pairs - 1)
                if within(i, 3, NT + 3):
                    l_cumulate(i - 3, 1 - u, (k4 - 3) % 4, 0)
                if u == 0 and within(i, 4, NT + 4):
                    l_turn_q(i - 3, (k4 - 3) % 4)
                if within(i, 5, NT + 5):
                    l_turn_y(i - 5, 1 - u)
                if within(i, 3, NT + 3):
                    l_cumulate(i - 3, 1 - u, (k4 - 3) % 4, 1)
                if u == 1 and within(i, 4, NT + 4):
                    l_before(i - 4, pairs - 2)
                if within(i, 0, NT):
                    l_turn(i, u)
                if within(i, 10, NT + 11):
                    l_route(i, u)
                if within(i, 5, NT + 5):
                    l_project(i - 5, 1 - u)
                if within(i, 3, NT + 3):
                    l_cumulate_k(i - 3, 1 - u, (k4 - 3) % 4)
            steady(pe, 12, 11, NT + 11, linear_attention, 4)

            wait(pe, rs("p_ready", 1), 1)
            for c in range(2):
                mm = pe.transpose(bank[5][:, c * P:(c + 1) * P], by_token[:, c * P:(c + 1) * P], ident_f)
            mm.then_inc(rs("p_turned", 1), 1)
            with pe.Fori(0, ROUNDS // 3) as m:
                for j in range(3):
                    wait(pe, rs("ge_ready", 1), 3 * m + j + 1)
                    pe.matmul(Cb[:, 0:4], same_b, counts[:, :], start=True, stop=True).then_inc(rs("cnt_ps", 1), 1)
            wait(pe, rs("f_ready", 1), 1)
            for f in range(2):
                for c in range(2):
                    mm = pe.transpose(bank[6][:, (2 * f + c) * P:(2 * f + c + 1) * P], flagsT[:, f, c * P:(c + 1) * P],
                                      ident_f)
            mm.then_inc(rs("f_turned", 1), 1)
            for n in range(3):
                ranks(1, n + 1)
            experts(1, F1)

        @block.scalar
        def _(act):
            act.preload_act_table(ACT.Exp)

            def copy_norm(b, u, tb):
                wait(act, S["pt_ps"], H0 * (b - 2) + 5 + tb)
                act.activation(nT[:, u, tb * P:(tb + 1) * P], PTb[:, 3 * P:4 * P], ACT.Copy).then_inc(S["nt_sb"], 1)

            def copy_v(b, u, tb):
                wait(act, S["g_full"], 6 * b + 5 + tb)
                act.activation(vv[:, u, tb, :], G[tb][:, :], ACT.Copy).then_inc(S["g_act"], 1)

            def exps(b, u, h):
                wait(act, S["max_done"], H0 * b + h + 1)
                wait(act, S["pt_ps"], H0 * b + h - 1)
                act.activation(pr[:, h % 2, 0, :], sneg[:, h % 2, 0, :], ACT.Exp, bias=mneg[:, u, h, 0:1], scale=-1.0,
                               accum_out=den[:, u, 0, h:h + 1])
                act.activation(pr[:, h % 2, 1:3, :], sneg[:, h % 2, 1:3, :], ACT.Exp, bias=mneg[:, u, h, 1:2], scale=-1.0,
                               accum_out=den[:, u, 1, h:h + 1]).then_inc(S["p_exp"], 1)

            def copy_probs(b, u, h):
                wait(act, S["pt_ps"], H0 * b + h + 1)
                wait(act, S["o_full"], H0 * b + h - 3)
                act.activation(pT[:, h % 4, :, :], PTb[:, 0:3 * P].rearrange("p (n t) -> p n t", n=3), ACT.Copy)\
                    .then_inc(S["pt_sb"], 1)

            def copy_route(b, tb):
                if within(b + 3, 0, B):
                    wait(act, S["pt_ps"], H0 * (b + 3) + tb + 1)
                else:
                    wait(act, rs("rt_ps", 0), 2 * (b + 3 - B) + tb + 1)
                if within(b + 3, 0, B + 2):
                    wait(act, S["proj_full"], b + 2)
                else:
                    wait(act, rs("lg_done", 0), b + 2 - B)
                act.activation(rnT[:, 0, tb * P:(tb + 1) * P], PTb[:, 3 * P:4 * P], ACT.Copy).then_inc(rs("rt_sb", 0), 1)

            def copy_attn(b, u, tb):
                wait(act, S["at_ps"], 2 * b + tb + 1)
                act.activation(aT[:, tb, :, :], Mb[:, :].rearrange("p (c t) -> p c t", c=NPAIR), ACT.Copy)\
                    .then_inc(S["at_sb"], 1)

            act.wait_ge(pool_const, 10)
            act.wait_ge(S["nt_ps"], 1)
            act.activation(nT[:, :, :], Mb[:, :].rearrange("p (u t) -> p u t", u=2), ACT.Copy).then_inc(S["nt_sb"], 2 * TB)
            copy_v(0, 0, 0)
            copy_v(0, 0, 1)

            def attention(b, u, turn):
                for h in range(H0):
                    if within(b, 0, B):
                        exps(b, u, h)
                    if h in (1, 2) and within(b, 3, B + 3):
                        copy_route(b - 3, h - 1)
                    if h in (5, 6) and within(b, 0, B - 2):
                        copy_norm(b + 2, u, h - 5)
                    if h >= 1:
                        if within(b, 0, B):
                            copy_probs(b, u, h - 1)
                    elif within(b, 1, B + 1):
                        copy_probs(b - 1, 1 - u, 7)
                    if within(b, 0, B - 1):
                        if h == 5:
                            copy_v(b + 1, 1 - u, 0)
                        if h == 6:
                            copy_v(b + 1, 1 - u, 1)
                    if within(b, 1, B + 1) and h in (3, 4):
                        copy_attn(b - 1, 1 - u, h - 3)
            steady(act, 4, 5, B + 3, attention)

            def softmax(r):
                act.wait_ge(rs("exp_in", r), 1)
                act.activation(rc[:, :, :], rb[:, :, :], ACT.Exp).then_inc(rs("exp_out", r), 1)

            def experts(r, F):
                C = F // P
                act.preload_act_table(ACT.Gelu)

                def across(k, n):
                    wait(act, rs("ft_ps", r), k + 1)
                    wait(act, rs("h_ps", r), k - 1)
                    act.activation(fnT[:, n % 2, :], bank[n % 2][:, 0:P], ACT.Copy).then_inc(rs("ft_sb", r), 1)

                def hidden(k, n):
                    u = n % 2
                    wait(act, rs("h_ps", r), k + 1)
                    wait(act, rs("y_ps", r), k - 1)
                    if r == 0:
                        for c in range(C):
                            ins = act.activation(hT[:, u, c * P:(c + 1) * P], bank[2 + u][:, c * P:(c + 1) * P], ACT.Gelu,
                                                 bias=wb[:, n, F + C * D + c:F + C * D + c + 1])
                    else:
                        ins = act.activation(hT[:, u, 0:F], bank[2 + u][:, 0:F], ACT.Gelu)
                    ins.then_inc(rs("h_sb", r), 1)

                def step(i, n, turn):
                    if within(i, 1, MAXT + 1):
                        across(i - 1, (n - 1) % RING)
                    if within(i, 2, MAXT + 2):
                        hidden(i - 2, (n - 2) % RING)
                steady(act, 2 * RING, 2, MAXT + 2, step, RING, 2)

            softmax(0)
            experts(0, F0)

            act.preload_act_table(ACT.Exp)

            def linear_attention(i, k4, turn):
                u = k4 % 2
                if within(i, 0, NT):
                    if isinstance(i, int) and i in (0, CH):
                        act.wait_ge(shift_known, 1 if i == 0 else NCH)
                    if isinstance(i, int):
                        wait(act, l["t_ps"], i - 1)
                    else:
                        wait_apart(act, l["t_ps"], i - 1, act_passed)
                    act.activation(ln[:, u, :], xt[:, bass.ds(i, 1), 0:D].rearrange("p o d -> p (o d)"), ACT.Identity,
                                   bias=shift[:, bass.ds(i, 1)], scale=xt[:, bass.ds(i, 1), RSTD]).then_inc(l["n"], 1)
                if within(i, 1, NT + 1):
                    k, v = i - 1, 1 - u
                    qkv = bank[6]
                    wait(act, l["qkv"], k + 1)
                    wait(act, l["phi"], k - 1)
                    act.activation(ex[:, v, :], qkv[:, 0:2 * D], ACT.Exp)
                    act.activation(rl[:, v, :], qkv[:, 0:2 * D], ACT.Relu).then_inc(l["relu"], 1)
                    wait(act, l["cum"], k - 3)
                    act.activation(lv[:, (k4 - 1) % 4, 0:D], qkv[:, 2 * D:3 * D], ACT.Copy).then_inc(l["v"], 1)
                if u == 0 and within(i, 4, NT + 4):
                    wait(act, l["q_ps"], (i - 2) // 2 if isinstance(i, int) else 2 * turn + k4 // 2 - 1)
                    act.activation(qT[:, :], bank[6][:, 3 * D:4 * D], ACT.Copy).then_inc(l["q_sb"], 1)
                if within(i, 7, NT + 7):
                    k, v = i - 7, (k4 - 7) % 4
                    wait_apart(act, l["res"], k + 1, act_passed)
                    act.activation(unused[:, 4, :], xt[:, bass.ds(k, 1), 0:D].rearrange("p o d -> p (o d)"), ACT.Copy,
                                   scale=1.0 / D, accum_out=lmean[:, v, :]).then_inc(l["mean"], 1)
                if within(i, 5, NT + 5):
                    k, v = i - 5, 1 - u
                    wait(act, l["yt_ps"], k + 1)
                    wait(act, l["pr"], k - 1)
                    act.activation(ylT[:, v, :], bank[7][:, P:2 * P], ACT.Copy).then_inc(l["yt_sb"], 1)
                if within(i, 7, NT + 7):
                    k, v = i - 7, (k4 - 7) % 4
                    wait_apart(act, l["mean"], k + 1, act_passed)
                    act.activation(unused[:, v, :], xt[:, bass.ds(k, 1), 0:D].rearrange("p o d -> p (o d)"), ACT.Square,
                                   bias=lmean[:, v, :], scale=-1.0, accum_out=lsq[:, v, :]).then_inc(l["squares"], 1)
                if within(i, 9, NT + 9):
                    k, v = i - 9, (k4 - 9) % 4
                    wait_apart(act, l["known"], k + 1, act_passed)
                    act.activation(rn[:, 1 - u, 0, :], xt[:, bass.ds(k, 1), 0:D].rearrange("p o d -> p (o d)"), ACT.Identity,
                                   bias=lshift[:, v, :], scale=lrstd[:, v, :]).then_inc(l["rn"], 1)
                if within(i, 10, NT + 11):
                    wait(act, l["route_ps"], i - 9)
                if within(i, 0, NT):
                    wait(act, l["t_ps"], i + 1)
                    wait(act, l["qkv"], i - 1)
                    act.activation(lnT[:, u, :], bank[7][:, 0:P], ACT.Copy).then_inc(l["t_sb"], 1)
                if within(i, 10, NT + 11):
                    if within(i, 10, NT + 10):
                        ins = act.activation(rnT[:, 0, u * P:(u + 1) * P], bank[7][:, 2 * P:3 * P], ACT.Copy)
                    if within(i, 11, NT + 11):
                        ins = act.activation(by_token[:, bass.ds((i - 11) * E, E)], bank[7][:, 3 * P:3 * P + E], ACT.Copy)
                    ins.then_inc(l["route_sb"], 1)
            steady(act, 12, 11, NT + 11, linear_attention, 4)

            softmax(1)
            experts(1, F1)

        @block.vector
        def _(dve):
            links = [0]

            def link(ins):
                links[0] += 1
                ins.then_inc(chain, 1)
                dve.wait_ge(chain, links[0])

            def stats_chunk(n, loaded):
                tiles = range(CH * (n % NCH), CH * (n % NCH + 1))
                dve.wait_ge(loaded[n % NCH], 16)
                for t in tiles:
                    last = dve.bn_stats(stats[:, t, :], xt[:, t, 0:D])
                link(last)
                for t in tiles:
                    last = dve.bn_aggr(mv[:, t, :], stats[:, t, :])
                last.then_inc(stats_done, 1)

            def normalise(dst, row):
                return dve.tensor_scalar(dst, row[:, 0:D], row[:, MEAN:MEAN + 1], row[:, RSTD:RSTD + 1],
                                         ALU.subtract, ALU.mult)

            stats_chunk(0, loaded_x)
            dve.wait_ge(rstd_known, 1)

            dve.wait_ge(loaded_c, 16)
            dve.tensor_copy(cb[:, :], cf[:, :])
            dve.wait_ge(pool_const, 10)

            def norm_rows(b, u):
                wait(dve, S["pt_ps"], H0 * (b - 4) + 6)
                for tb in range(TB):
                    ins = normalise(n_tok[:, u, tb, :], xt_row(TB * b + tb))
                ins.then_inc(S["n_ready"], 1)

            def xt_row(t):
                return xt[:, t, :]

            def add_pos(b, u, use):
                wait(dve, S["g_full"], 6 * b + use + 1)
                ps = G[use % 2][:, :].rearrange("p (j t) -> p j t", j=2)
                pair0 = 2 * (use // 2)
                if use % 2:
                    dve.tensor_tensor(kp[:, u, pair0:pair0 + 2, :], ps, bc(pos_sb[:, 0:1, :], [P, 2, T]), ALU.add)\
                        .then_inc(S["g_dve"], 1)
                else:
                    for half in range(2):
                        rows = slice(64 * half, 64 * half + 64)
                        h0 = 2 * pair0 + half
                        ins = dve.scalar_tensor_tensor(out=qz[rows, u, h0:h0 + 3:2, :], in0=ps[rows], scalar=SCALE0,
                                                       in1=bc(pos_sb[rows, 1:2, :], [64, 2, T]), op0=ALU.mult, op1=ALU.add)
                    ins.then_inc(S["g_dve"], 1)

            def row_max(b, u, h):
                wait(dve, S["p_exp"], H0 * b + h - 1)
                wait_apart(dve, S["s_full"], H0 * b + h + 1, dve_passed)
                for tb in range(TB):
                    ins = dve.tensor_tensor_reduce(sneg[:, h % 2, tb:2 * tb + 1, :].rearrange("p n s -> p (n s)"),
                                                   Sb[h % 2][:, tb * P:(2 * tb + 1) * P], masks[tb], -1.0, -NEG,
                                                   ALU.add, ALU.min, mneg[:, u, h, tb:tb + 1])
                ins.then_inc(S["max_done"], 1)

            def divide(b, u):
                wait(dve, S["o_full"], H0 * (b + 1))
                dve.reciprocal(rden[:, :, :], den[:, u, :, :]).then_inc(S["r_done"], 1)
                wait(dve, S["r_done"], b + 1)
                for tb in range(TB):
                    ins = dve.tensor_tensor(attn[:, u, tb, :].rearrange("p (h d) -> p h d", h=H0),
                                            Ob[tb][:, :].rearrange("p (h d) -> p h d", h=H0),
                                            bc(rden[:, tb, :, None], [P, H0, DH0]), ALU.mult)
                ins.then_inc(S["an_done"], 1)

            def route_stats(b, u):
                wait_apart(dve, S["res_done"], b + 1, dve_passed)
                for tb in range(TB):
                    ins = dve.bn_stats(st2[:, u, tb, :], xt_row(TB * b + tb)[:, 0:D])
                ins.then_inc(rs("bn_done", 0), 1)

            def route_mean(b, u):
                wait(dve, rs("norm_known", 0), b - 1)
                wait_apart(dve, rs("bn_done", 0), b + 1, dve_passed)
                for tb in range(TB):
                    ins = dve.bn_aggr(mv2[:, u, tb, :], st2[:, u, tb, :])
                ins.then_inc(rs("mv_done", 0), 1)

            def route_rows(b, u):
                wait(dve, rs("norm_known", 0), b + 1)
                if within(b + 2, 0, B + 1):
                    wait(dve, S["pt_ps"], H0 * (b + 1) + 2)
                else:
                    wait(dve, rs("rt_ps", 0), 2)
                for tb in range(TB):
                    ins = normalise(rn[:, u, tb, :], xt_row(TB * b + tb))
                ins.then_inc(rs("rn_ready", 0), 1)

            def keep_logits(b):
                if within(b + 3, 0, B + 1):
                    wait(dve, S["proj_full"], b + 3)
                else:
                    wait(dve, rs("lg_done", 0), b + 3 - B)
                ins = dve.tensor_copy(by_token[:, bass.ds(TB * E * b, TB * E)], Mb[:, T:T + TB * E])
                if not within(b + 3, 0, B + 1):
                    ins.then_inc(rs("lg_copied", 0), 1)

            def residual(b, u):
                wait(dve, S["proj_full"], b + 1)
                rows = xt[:, bass.ds(TB * b, TB), 0:D]
                dve.tensor_tensor(rows, Mb[:, 0:TB * D].rearrange("p (t d) -> p t d", t=TB), rows, ALU.add)\
                    .then_inc(S["res_done"], 1)

            norm_rows(0, 0)
            norm_rows(1, 1)
            dve.wait_ge(loaded_a, 16 * 2)
            for use in range(4):
                add_pos(0, 0, use)

            early = [(0, 5), (1, 2), (1, 6)]
            def attention(b, u, turn):
                for h in range(H0):
                    if within(b, 0, B):
                        row_max(b, u, h)
                    if h == 1 and within(b, 1, B + 1):
                        divide(b - 1, 1 - u)
                    if 1 <= h <= 4 and within(b, 0, B - 1):
                        add_pos(b + 1, 1 - u, h - 1)
                    if h == 3 and within(b, 0, B - 2):
                        if isinstance(b, int) and b == 2:
                            dve.wait_ge(rstd_known, NCH)
                        norm_rows(b + 2, u)
                    if isinstance(b, int) and (b, h) in early:
                        stats_chunk(early.index((b, h)) + 1, loaded_x)
                    if within(b, 2, B + 2):
                        if h == 4:
                            route_stats(b - 2, u)
                        if h == 5:
                            route_mean(b - 2, u)
                        if h == 7:
                            route_rows(b - 2, u)
                    if h == 0 and within(b, 4, B + 4):
                        keep_logits(b - 4)
                    if h == 0 and within(b, 2, B + 2):
                        residual(b - 2, u)
            steady(dve, 4, 6, B + 4, attention)
            dve.wait_ge(rs("lg_copied", 0), 2)

            Lb, Rb, Cb = bank[2], bank[3], bank[4]
            FULL = [P, E, NT]

            def over_e(a):
                return a.rearrange("p e t -> p t e")

            def per_token(a):
                return bc(a[:, None, :], FULL)

            def per_expert(a):
                return bc(a[:, :, None], FULL)

            def logits(r):
                ps = by_token[:, :].rearrange("p (t e) -> p e t", e=E)
                if r == 0:
                    link(dve.tensor_tensor(lg[:, :, :], ps, per_expert(br_sb[:, :]), ALU.add))
                else:
                    link(dve.tensor_copy(lg[:, :, :], ps))
                link(dve.tensor_reduce(tm[:, :], over_e(lg[:, :, :]), AX.X, ALU.max))
                dve.tensor_tensor(rb[:, :, :], lg[:, :, :], per_token(tm[:, :]), ALU.subtract).then_inc(rs("exp_in", r), 1)

            def first_equal(values):
                link(dve.tensor_tensor(ra[:, :, :], values, per_token(tm[:, :]), ALU.is_equal))
                link(dve.tensor_tensor(ra[:, :, :], ra[:, :, :], per_expert(ewt[:, :]), ALU.mult))
                link(dve.tensor_reduce(tn[:, :], over_e(ra[:, :, :]), AX.X, ALU.max))
                link(dve.tensor_tensor(oh[:, :, :], ra[:, :, :], per_token(tn[:, :]), ALU.is_equal))

            def flags_ranked(flags, r, n):
                dve.tensor_copy(ohb[:, :, :], flags).then_inc(rs("oh_ready", r), 1)
                dve.wait_ge(rs("rank_ps", r), n)
                tot = Rb[:, E * NT:2 * E * NT].rearrange("p (e t) -> p e t", e=E)
                rank = Rb[:, 0:E * NT].rearrange("p (e t) -> p e t", e=E)
                flat = "p e t -> p (e t)"
                link(dve.tensor_tensor_scan(rb[:, :, :].rearrange(flat), tile0[:, :, :].rearrange(flat),
                                            Rb[:, E * NT:2 * E * NT], 0.0, ALU.mult, ALU.add))
                link(dve.tensor_copy(cnt[:, :], rb[:, :, NT - 1]))
                link(dve.tensor_tensor(rd[:, :, :], rb[:, :, :], tot, ALU.subtract))
                link(dve.tensor_tensor(rd[:, :, :], rd[:, :, :], rank, ALU.add))

            def give_slots(r, n):
                flags_ranked(oh[:, :, :], r, n)
                link(dve.tensor_scalar(cnti[:, :], cnt[:, :], float(P - 1), None, ALU.add))
                link(dve.tensor_scalar(cnti[:, :], cnti[:, :], 7, 7, ALU.arith_shift_right, ALU.arith_shift_left))
                link(dve.tensor_copy(padc[:, :], cnti[:, :]))
                link(dve.tensor_tensor_scan(ends[:, :], one8[:, :], padc[:, :], 0.0, ALU.mult, ALU.add))
                link(dve.tensor_tensor(base[:, :], ends[:, :], padc[:, :], ALU.subtract))
                link(dve.tensor_tensor(rd[:, :, :], rd[:, :, :], per_expert(base[:, :]), ALU.add))
                link(dve.tensor_tensor(rd[:, :, :], rd[:, :, :], oh[:, :, :], ALU.mult))
                link(dve.tensor_reduce(tn[:, :], over_e(rd[:, :, :]), AX.X, ALU.add))
                dve.tensor_copy(slots[:, :], tn[:, :]).then_inc(rs("slot_ready", r), 1)
                link(dve.tensor_tensor(tcmp[:, :, :], bc(ends[:, None, :], [P, MAXT, E]), bc(k128[:, :, None], [P, MAXT, E]),
                                       ALU.is_le))
                link(dve.tensor_reduce(tef[:, :], tcmp[:, :, :], AX.X, ALU.add))
                link(dve.tensor_scalar(te[:, :], tef[:, :], float(E - 1), None, ALU.min))

            def experts(r, F, width, weights):
                C = F // P

                def prepare(k, n, turn, expert):
                    wait(dve, row_in[r][n], 16 * (turn + 1))
                    wait(dve, rs("ft_ps", r), k - 1)
                    normalise(fn[:, n % 2, :], xr[:, n, :]).then_inc(rs("fn_ready", r), 1)
                    wait(dve, rs("y_ps", r), k - RING + 1)
                    dve.tensor_copy(wb[:, n, 0:width], weights[:, bass.ds(expert, 1), :].rearrange("p o c -> p (o c)"))\
                        .then_inc(rs("w_copied", r), 1)

                def finish(k, n, turn):
                    wait(dve, rs("y_ps", r), k + 1)
                    wait(dve, y_sent[r][(n - 3) % RING], 16 * (turn + 1 if n >= 3 else turn))
                    y = bank[4 + n % 2][:, 0:D]
                    if r == 0:
                        b2 = F + C * D + C
                        dve.tensor_tensor(yb[:, n % 2, :], y, wb[:, n, b2:b2 + D], ALU.add).then_inc(yb_ready, 1)
                        wait(dve, yb_ready, k + 1)
                        y = yb[:, n % 2, :]
                    dve.tensor_copy(ids[:, n % 3, :], xr[:, n, ID:ID + 1].bitcast(i32))
                    dve.scalar_tensor_tensor(out=yo[:, n % 3, :], in0=y, scalar=xr[:, n, GATE:GATE + 1],
                                             in1=xr[:, n, 0:D], op0=ALU.mult, op1=ALU.add).then_inc(rs("y_out", r), 1)

                def step(i, n, turn):
                    if within(i, 0, MAXT):
                        expert = dve.value_load(te[0:1, bass.ds(i, 1)], min_val=0, max_val=E - 1)
                    if within(i, 4, MAXT + 4):
                        finish(i - 4, (n - 4) % RING, turn if n >= 4 else turn - 1)
                    if within(i, 0, MAXT):
                        prepare(i, n, turn, expert)
                steady(dve, 2 * RING, 4, MAXT + 4, step, RING, 2)

            dve.wait_ge(loaded_w, 16 * 9)
            logits(0)
            first_equal(lg[:, :, :])
            dve.wait_ge(rs("exp_out", 0), 1)
            link(dve.tensor_reduce(tn[:, :], over_e(rc[:, :, :]), AX.X, ALU.add))
            link(dve.reciprocal(xt[:, :, GATE], tn[:, :]))
            give_slots(0, 1)
            dve.wait_ge(rs("slot_ready", 0), 1)
            experts(0, F0, W0R, w0_sb)

            stats_chunk(NCH, reloaded)

            def l_features(k, u, k4):
                wait(dve, l["relu"], k + 1)
                wait(dve, l["cum"], k - 2)
                dve.scalar_tensor_tensor(out=ph[:, k4, :], in0=ex[:, u, :], scalar=1.0, in1=rl[:, u, :],
                                         op0=ALU.min, op1=ALU.add).then_inc(l["phi"], 1)

            def l_query(k, u, k4, c):
                if c == 0:
                    wait(dve, l["cum"], k + 1)
                    wait(dve, l_red, k)
                q = ph[:, k4, 0:D].rearrange("p (h i) -> p h i", h=H1)
                hs = slice(c * H1 // 2, (c + 1) * H1 // 2)
                shape = [P, H1 // 2, DH1, DH1]
                state = bank[2 + 2 * u + c][:, :].rearrange("p (h i j) -> p h i j", h=H1 // 2, i=DH1)
                o = qs[:, c * 512:(c + 1) * 512].rearrange("p (h j i) -> p h i j", h=H1 // 2, i=DH1)
                dve.tensor_tensor(o, state, bc(q[:, hs, :, None], shape), ALU.mult)

            def l_query_k(k, u, k4, pair):
                if u == 0:
                    wait(dve, l["before"], pair)
                    dve.tensor_tensor(total[:, :], bank[0][:, 2 * P:2 * P + D + H1], heads_f, ALU.mult)
                dve.tensor_tensor(qs[:, KV:KV + D], bank[u][:, 0:P], ph[:, k4, 0:D], ALU.mult).then_inc(l["mul"], 1)

            def l_sum(k):
                wait(dve, l["mul"], k + 1)
                wait(dve, l["y"], k)
                dve.tensor_reduce(num[:, :], qs[:, :].rearrange("p (g i) -> p g i", i=DH1), AX.X, ALU.add).then_inc(l_red, 1)

            def l_join(k, pair):
                wait(dve, l_red, k + 1)
                wait(dve, l["before"], pair + 1)
                dve.tensor_tensor(num2[:, :], bank[1][:, 2 * P:2 * P + D + H1], num[:, :], ALU.add).then_inc(l["joined"], 1)

            def l_eps_added(k, u, pair):
                if u == 1:
                    wait(dve, l["joined"], pair + 1)
                else:
                    wait(dve, l_red, k + 1)
                dve.tensor_scalar(lden[:, :], (num, num2)[u][:, D:D + H1], LA_EPS, None, ALU.add).then_inc(l_eps, 1)

            def l_reciprocal(k):
                wait(dve, l_eps, k + 1)
                dve.reciprocal(rdn[:, :], lden[:, :]).then_inc(l_rec, 1)

            def l_divide(k, u):
                wait(dve, l_rec, k + 1)
                wait(dve, l["yt_ps"], k - 1)
                dve.tensor_tensor(yl[:, u, :].rearrange("p (h j) -> p h j", h=H1),
                                  (num, num2)[u][:, 0:D].rearrange("p (h j) -> p h j", h=H1),
                                  bc(rdn[:, :, None], [P, H1, DH1]), ALU.mult).then_inc(l["y"], 1)

            def l_residual(k, u):
                wait(dve, l["pr"], k + 1)
                row = xt_row(k)
                dve.tensor_tensor(row[:, 0:D], bank[u][:, P:2 * P], row[:, 0:D], ALU.add).then_inc(l["res"], 1)

            def linear_attention(i, k4, turn):
                u = k4 % 2
                pairs = i // 2 if isinstance(i, int) else 2 * turn + k4 // 2
                if within(i, 4, NT + 4):
                    l_query(i - 4, u, k4, 0)
                if within(i, 5, NT + 5):
                    l_reciprocal(i - 5)
                if within(i, 4, NT + 4):
                    l_query(i - 4, u, k4, 1)
                if within(i, 5, NT + 5):
                    l_divide(i - 5, 1 - u)
                if within(i, 4, NT + 4):
                    l_query_k(i - 4, u, k4, pairs - 2)
                if u == 1 and within(i, 6, NT + 6):
                    l_residual(i - 6, u)
                if within(i, 2, NT + 2):
                    l_features(i - 2, u, (k4 - 2) % 4)
                if within(i, 4, NT + 4):
                    l_sum(i - 4)
                if u == 1 and within(i, 4, NT + 4):
                    l_join(i - 4, pairs - 2)
                if u == 0 and within(i, 6, NT + 6):
                    l_residual(i - 6, u)
                if within(i, 4, NT + 4):
                    l_eps_added(i - 4, u, pairs - 2)
                if isinstance(i, int) and 1 <= i < NCH:
                    stats_chunk(NCH + i, reloaded)
            steady(dve, 12, 6, NT + 6, linear_attention, 4)
            dve.wait_ge(l["res"], NT)

            dve.wait_ge(l["route_sb"], NT + 1)
            logits(1)
            dve.wait_ge(rs("exp_out", 1), 1)
            link(dve.tensor_reduce(tn[:, :], over_e(rc[:, :, :]), AX.X, ALU.add))
            link(dve.reciprocal(tm[:, :], tn[:, :]))
            link(dve.tensor_tensor(lg[:, :, :], rc[:, :, :], per_token(tm[:, :]), ALU.mult))
            dve.tensor_copy(by_token[:, :].rearrange("p (t e) -> p e t", e=E), lg[:, :, :]).then_inc(rs("p_ready", 1), 1)
            dve.wait_ge(rs("p_turned", 1), 1)
            link(dve.tensor_copy(lgT[:, :], bank[5][:, 0:2 * P]))
            dve.memset(counts[:, :], float(2 * P))
            link(dve.memset(thr[:, :], 0))

            def search_round(n, done):
                def step(ins, j):
                    ins.then_inc(search, 1)
                    dve.wait_ge(search, done + j)
                step(dve.tensor_tensor(cand[:, :], bits_sb[:, bass.ds(n, 1), :].rearrange("p o j -> p (o j)"),
                                       bc(thr[:, 0:1], [P, 4]), ALU.bitwise_or), 1)
                for j in range(3):
                    ins = dve.tensor_scalar(geT[:, j, :], lgT[:, :], cand[:, j:j + 1].bitcast(fp32), None, ALU.is_ge,
                                            ALU.add, accum_out=counts[:, j:j + 1])
                ins.then_inc(rs("ge_ready", 1), 1)
                dve.wait_ge(rs("cnt_ps", 1), n + 1)
                step(dve.scalar_tensor_tensor(out=passed[:, :], in0=Cb[:, 0:4], scalar=float(CAP),
                                              in1=cand[:, :].bitcast(fp32), op0=ALU.is_ge, op1=ALU.mult), 2)
                step(dve.tensor_reduce(thr[:, :].bitcast(fp32), passed[:, :], AX.X, ALU.max), 3)
            with dve.Fori(0, ROUNDS // 3) as m:
                for j in range(3):
                    search_round(3 * m + j, 9 * m + 3 * j)
            dve.tensor_scalar(flagsT[:, 0, :], lgT[:, :], thr[:, 0:1].bitcast(fp32), None, ALU.is_gt)
            dve.tensor_scalar(flagsT[:, 1, :], lgT[:, :], thr[:, 0:1].bitcast(fp32), None, ALU.is_equal)\
                .then_inc(rs("f_ready", 1), 1)
            dve.wait_ge(rs("f_turned", 1), 1)
            above, at = [bank[6][:, f * 2 * P:(f + 1) * 2 * P].rearrange("p (t e) -> p e t", e=E) for f in range(2)]
            dve.tensor_copy(ohb[:, :, :], above).then_inc(rs("oh_ready", 1), 1)
            link(dve.tensor_copy(rc[:, :, :], above))
            link(dve.tensor_copy(oh[:, :, :], at))
            dve.wait_ge(rs("rank_ps", 1), 1)
            link(dve.tensor_reduce(cnt[:, :], Rb[:, E * NT:2 * E * NT].rearrange("p (e t) -> p e t", e=E), AX.X, ALU.add))
            link(dve.tensor_scalar(need[:, :], cnt[:, :], -1.0, float(CAP), ALU.mult, ALU.add))
            flags_ranked(oh[:, :, :], 1, 2)
            link(dve.tensor_tensor(rd[:, :, :], rd[:, :, :], per_expert(need[:, :]), ALU.is_lt))
            link(dve.tensor_tensor(rd[:, :, :], rd[:, :, :], oh[:, :, :], ALU.mult))
            link(dve.tensor_tensor(rc[:, :, :], rc[:, :, :], rd[:, :, :], ALU.add))
            link(dve.tensor_reduce(tm[:, :], over_e(rc[:, :, :]), AX.X, ALU.max))
            link(dve.tensor_scalar(tm[:, :], tm[:, :], -1.0, 1.0, ALU.mult, ALU.add))
            link(dve.tensor_tensor(rc[:, :, :], rc[:, :, :], per_token(tm[:, :]), ALU.max))
            link(dve.tensor_tensor(ra[:, :, :], lg[:, :, :], rc[:, :, :], ALU.mult))
            link(dve.scalar_tensor_tensor(out=rb[:, :, :], in0=rc[:, :, :], scalar=-1.0, in1=ra[:, :, :],
                                          op0=ALU.add, op1=ALU.add))
            link(dve.tensor_reduce(tm[:, :], over_e(rb[:, :, :]), AX.X, ALU.max))
            link(dve.tensor_copy(xt[:, :, GATE], tm[:, :]))
            first_equal(rb[:, :, :])
            give_slots(1, 3)
            dve.wait_ge(rs("slot_ready", 1), 1)
            experts(1, F1, W1R, w1_sb)


def _constants():
    f = np.float32
    i, j = np.arange(P)[:, None], np.arange(P)[None, :]
    mats = [i == j, i <= j, i < j, np.ones((P, P)), i % E == j % E, np.zeros((P, P)), np.where(j > i, NEG, 0.0), i // DH1 == j // DH1,
            i // DH1 == j[:, 0:H1]]
    consts = np.concatenate([np.asarray(m, f) for m in mats], axis=1)
    pos = np.arange(T, dtype=f)[:, None]
    div = np.exp(np.arange(0, DH0, 2, dtype=f) * f(-np.log(10000.0) / DH0))
    ang = pos * div
    pe = np.stack([np.sin(ang), np.cos(ang)], axis=-1).reshape(T, DH0).T
    pos2 = np.concatenate([pe, pe], axis=0).astype(f)
    return consts, np.stack([pos2, pos2 * f(SCALE0)], axis=1)


def _layout(a):
    consts, pos = _constants()
    w = np.asarray(a["L0_attn_Wqkv"]).reshape(H0, 3, DH0, D)
    wqkv = np.ascontiguousarray(w.transpose(3, 1, 0, 2).reshape(D, 3 * H0 * DH0))
    wo = np.ascontiguousarray(np.asarray(a["L0_attn_Wo"]).T.reshape(NPAIR, P, D).transpose(1, 0, 2))

    def rows(m, c):
        return np.asarray(m).reshape(E, c, P, D).transpose(2, 0, 1, 3).reshape(P, E, c * D)
    w0 = np.concatenate([
        np.asarray(a["L0_ffn_W1"]).transpose(1, 0, 2),
        rows(a["L0_ffn_W2"], C0),
        np.asarray(a["L0_ffn_b1"]).reshape(E, C0, P).transpose(2, 0, 1),
        np.broadcast_to(np.asarray(a["L0_ffn_b2"])[None], (P, E, D)),
    ], axis=2)
    w1 = np.concatenate([np.asarray(a["L1_ffn_W1"]).transpose(1, 0, 2), rows(a["L1_ffn_W2"], C1)], axis=2)
    return dict(
        x=np.asarray(a["L0_attn_x"]).reshape(NTOK, D), consts=consts, pos=pos, wqkv=wqkv, wo=wo, w0=w0,
        wr=np.asarray(a["L0_ffn_Wr"]), br=np.ascontiguousarray(np.broadcast_to(np.asarray(a["L0_ffn_br"])[None], (P, E))),
        wattn=np.asarray(a["L1_attn_w_attn"]), wproj=np.asarray(a["L1_attn_w_proj"]), wg=np.asarray(a["L1_ffn_Wg"]), w1=w1,
        bits=np.ascontiguousarray(np.broadcast_to(
            (np.array([1, 2, 3, 0])[None] << np.arange(2 * ROUNDS - 2, -1, -2)[:, None]).astype(np.int32)[None], (P, ROUNDS, 4))))


def kernel(**inputs):
    import concourse.bacc as bacc
    from concourse.bass_utils import run_bass_kernel_spmd as run

    nc = bacc.Bacc("TRN2", target_bir_lowering=False, num_devices=1)
    arrays = {f"in_{k}": np.ascontiguousarray(v) for k, v in _layout(inputs).items()}
    args = [nc.dram_tensor(k, v.shape, mybir.dt.from_np(v.dtype), kind="ExternalInput").ap() for k, v in arrays.items()]
    out = nc.dram_tensor("out", (NTOK, D), mybir.dt.float32, kind="ExternalOutput").ap()
    build_model(nc, *args, out)
    r = run(nc, [arrays], core_ids=[0])
    return r.results[0]["out"].reshape(B, T, D)
```
